# Optimizing a Trainium2 kernel written in Bass

```python
import numpy as np
import jax
import jax.numpy as jnp

def _softmax(x, axis=-1):
    return jax.nn.softmax(x, axis=axis)

def _gelu(x):
    return jax.nn.gelu(x, approximate=True)

def _silu(x):
    return jax.nn.silu(x)

def _sigmoid(x):
    return jax.nn.sigmoid(x)

def _layernorm(x, axis=-1, eps=1e-05):
    m = jnp.mean(x, axis=axis, keepdims=True)
    v = jnp.var(x, axis=axis, keepdims=True)
    return (x - m) / jnp.sqrt(v + eps)

def _scatter_add(tgt, idx, src, axis=0):
    return tgt.at[idx].add(src)

def _segment_sum(src, seg, n):
    return jax.ops.segment_sum(src, seg, n)
kernel_name = 'mk_gnn_preln_d2_gnn_r8_134624'

def setup_inputs(seed: int=0):
    np.random.seed(seed)
    _w = jnp.asarray

    def _rec_inputs():
        import jax
        import jax.numpy as jnp
        _gk = jax.random.key(seed)
        x = -0.000202 + 1 * jax.random.normal(jax.random.fold_in(_gk, 1), (12500, 64), jnp.float32)
        _s = jax.random.randint(jax.random.fold_in(_gk, 2), (200000,), 0, 12500, jnp.int32)
        _d = jax.random.randint(jax.random.fold_in(_gk, 3), (200000,), 0, 12500, jnp.int32)
        _loop = jnp.arange(12500, dtype=jnp.int32)
        src = jnp.concatenate([_s, _d, _loop])
        dst = jnp.concatenate([_d, _s, _loop])
        _o = jnp.argsort(dst, stable=True)
        src = src[_o]
        dst = dst[_o]
        edge_weight1 = jax.random.uniform(jax.random.fold_in(_gk, 13), (412500, 1), jnp.float32, 0.0, 0.999999)
        return (x, src, dst, edge_weight1)
    x, src, dst, edge_weight1 = _rec_inputs()

    def _L0_gnn_setup():
        import jax, jax.numpy as jnp
        import numpy as np
        NUM_NODES = 12500
        NUM_HYPEREDGES = 25000
        NNZ = 150000
        IN_DIM = 64
        HID_DIM = 64
        OUT_DIM = 64

        def _hypergraph_conv(x, node_idx, edge_idx, D_inv, B_inv, W, b):
            xt = x @ W
            e = B_inv[:, None] * jax.ops.segment_sum(xt[node_idx], edge_idx, num_segments=NUM_HYPEREDGES)
            out = D_inv[:, None] * jax.ops.segment_sum(e[edge_idx], node_idx, num_segments=NUM_NODES)
            return out + b
        key = jax.random.key(seed)
        k1, k2, k3, k4, k5, k6, k7, k8 = jax.random.split(key, 8)
        x = jax.random.normal(k1, (NUM_NODES, IN_DIM), dtype=jnp.float32)
        node_idx = jax.random.randint(k2, (NNZ,), 0, NUM_NODES, dtype=jnp.int64)
        edge_idx = jax.random.randint(k3, (NNZ,), 0, NUM_HYPEREDGES, dtype=jnp.int64)
        hyperedge_index = jnp.stack([node_idx, edge_idx], axis=0)
        s1 = 1.0 / np.sqrt(IN_DIM)
        s2 = 1.0 / np.sqrt(HID_DIM)
        W1 = jax.random.uniform(k4, (IN_DIM, HID_DIM), jnp.float32, -s1, s1)
        b1 = jax.random.uniform(k5, (HID_DIM,), jnp.float32, -s1, s1)
        W2 = jax.random.uniform(k6, (HID_DIM, OUT_DIM), jnp.float32, -s2, s2)
        b2 = jax.random.uniform(k7, (OUT_DIM,), jnp.float32, -s2, s2)
        return {'x': x, 'hyperedge_index': hyperedge_index, 'W1': W1, 'b1': b1, 'W2': W2, 'b2': b2}
    _L0_gnn_all = _L0_gnn_setup()
    _L0_gnn_in = {k: v for k, v in _L0_gnn_all.items() if k in ('W1', 'b1', 'W2', 'b2')}
    del _L0_gnn_all

    def _L1_gnn_setup():
        import jax, jax.numpy as jnp
        import numpy as np
        N_NODES = 6250
        N_EDGES = 100000
        NODE_NF = 64
        HIDDEN_NF = 128

        def _linear_params(key, fan_in, fan_out):
            kw, kb = jax.random.split(key)
            bound = 1.0 / np.sqrt(fan_in)
            W = jax.random.uniform(kw, (fan_in, fan_out), minval=-bound, maxval=bound, dtype=jnp.float32)
            b = jax.random.uniform(kb, (fan_out,), minval=-bound, maxval=bound, dtype=jnp.float32)
            return (W, b)
        key = jax.random.key(seed)
        ks = jax.random.split(key, 8)
        h = jax.random.normal(ks[0], (N_NODES, NODE_NF), dtype=jnp.float32)
        row = jax.random.randint(ks[1], (N_EDGES,), 0, N_NODES)
        col = jax.random.randint(ks[2], (N_EDGES,), 0, N_NODES)
        dist = jax.random.uniform(ks[3], (N_EDGES, 1), dtype=jnp.float32)
        eW1, eb1 = _linear_params(ks[4], 2 * NODE_NF + 1, HIDDEN_NF)
        eW2, eb2 = _linear_params(ks[5], HIDDEN_NF, HIDDEN_NF)
        nW1, nb1 = _linear_params(ks[6], HIDDEN_NF + NODE_NF, HIDDEN_NF)
        nW2, nb2 = _linear_params(ks[7], HIDDEN_NF, NODE_NF)
        return {'h': h, 'row': row, 'col': col, 'dist': dist, 'eW1': eW1, 'eb1': eb1, 'eW2': eW2, 'eb2': eb2, 'nW1': nW1, 'nb1': nb1, 'nW2': nW2, 'nb2': nb2}
    _L1_gnn_all = _L1_gnn_setup()
    _L1_gnn_in = {k: v for k, v in _L1_gnn_all.items() if k in ('eW1', 'eb1', 'eW2', 'eb2', 'nW1', 'nb1', 'nW2', 'nb2')}
    del _L1_gnn_all
    return {'x': x, 'src': src, 'dst': dst, 'edge_weight1': edge_weight1, 'L0_gnn_W1': _L0_gnn_in['W1'], 'L0_gnn_b1': _L0_gnn_in['b1'], 'L0_gnn_W2': _L0_gnn_in['W2'], 'L0_gnn_b2': _L0_gnn_in['b2'], 'L1_gnn_eW1': _L1_gnn_in['eW1'], 'L1_gnn_eb1': _L1_gnn_in['eb1'], 'L1_gnn_eW2': _L1_gnn_in['eW2'], 'L1_gnn_eb2': _L1_gnn_in['eb2'], 'L1_gnn_nW1': _L1_gnn_in['nW1'], 'L1_gnn_nb1': _L1_gnn_in['nb1'], 'L1_gnn_nW2': _L1_gnn_in['nW2'], 'L1_gnn_nb2': _L1_gnn_in['nb2']}

def reference(x, src, dst, edge_weight1, L0_gnn_W1, L0_gnn_b1, L0_gnn_W2, L0_gnn_b2, L1_gnn_eW1, L1_gnn_eb1, L1_gnn_eW2, L1_gnn_eb2, L1_gnn_nW1, L1_gnn_nb1, L1_gnn_nW2, L1_gnn_nb2):
    import jax
    import jax.numpy as jnp

    def _L0_gnn_ref(x, hyperedge_index, W1, b1, W2, b2):
        import jax, jax.numpy as jnp
        import numpy as np
        NUM_NODES = 12500
        NUM_HYPEREDGES = 25000
        NNZ = 150000
        IN_DIM = 64
        HID_DIM = 64
        OUT_DIM = 64

        def _hypergraph_conv(x, node_idx, edge_idx, D_inv, B_inv, W, b):
            xt = x @ W
            e = B_inv[:, None] * jax.ops.segment_sum(xt[node_idx], edge_idx, num_segments=NUM_HYPEREDGES)
            out = D_inv[:, None] * jax.ops.segment_sum(e[edge_idx], node_idx, num_segments=NUM_NODES)
            return out + b
        node_idx = hyperedge_index[0]
        edge_idx = hyperedge_index[1]
        ones = jnp.ones((node_idx.shape[0],), dtype=x.dtype)
        D = jax.ops.segment_sum(ones, node_idx, num_segments=NUM_NODES)
        B = jax.ops.segment_sum(ones, edge_idx, num_segments=NUM_HYPEREDGES)
        D_inv = jnp.where(D > 0, 1.0 / D, 0.0)
        B_inv = jnp.where(B > 0, 1.0 / B, 0.0)
        h = jax.nn.relu(_hypergraph_conv(x, node_idx, edge_idx, D_inv, B_inv, W1, b1))
        y = _hypergraph_conv(h, node_idx, edge_idx, D_inv, B_inv, W2, b2)
        return y

    def _L1_gnn_ref(h, row, col, dist, eW1, eb1, eW2, eb2, nW1, nb1, nW2, nb2):
        import jax, jax.numpy as jnp
        import numpy as np
        N_NODES = 6250
        N_EDGES = 100000
        NODE_NF = 64
        HIDDEN_NF = 128

        def _linear_params(key, fan_in, fan_out):
            kw, kb = jax.random.split(key)
            bound = 1.0 / np.sqrt(fan_in)
            W = jax.random.uniform(kw, (fan_in, fan_out), minval=-bound, maxval=bound, dtype=jnp.float32)
            b = jax.random.uniform(kb, (fan_out,), minval=-bound, maxval=bound, dtype=jnp.float32)
            return (W, b)
        edge_in = jnp.concatenate([h[row], h[col], dist], axis=1)
        e = jax.nn.silu(edge_in @ eW1 + eb1)
        e = jax.nn.silu(e @ eW2 + eb2)
        agg = jax.ops.segment_sum(e, row, num_segments=h.shape[0])
        node_in = jnp.concatenate([h, agg], axis=1)
        out = jax.nn.silu(node_in @ nW1 + nb1) @ nW2 + nb2
        return out
    edge_index = jnp.stack([src, dst])
    h = jnp.maximum(_layernorm(x, axis=-1), 0.0)
    x = x + _L0_gnn_ref(h, edge_index, L0_gnn_W1, L0_gnn_b1, L0_gnn_W2, L0_gnn_b2)
    h = jnp.maximum(_layernorm(x, axis=-1), 0.0)
    x = x + _L1_gnn_ref(h, src, dst, edge_weight1, L1_gnn_eW1, L1_gnn_eb1, L1_gnn_eW2, L1_gnn_eb2, L1_gnn_nW1, L1_gnn_nb1, L1_gnn_nW2, L1_gnn_nb2)
    return x

_drawn_inputs = setup_inputs


def setup_inputs(seed=0):
    import zlib

    import numpy as np

    out = dict(_drawn_inputs(seed))
    spreads = {}
    factors = {'edge_weight1': 32.669, 'L1_gnn_nb1': 4.384}
    for name, (base, spread) in spreads.items():
        noise = np.random.default_rng([zlib.crc32(name.encode()), seed]).standard_normal(out[name].shape)
        drawn = base * np.exp(spread * noise) if base else spread * noise
        out[name] = jnp.asarray(drawn.astype(out[name].dtype))
    for name, factor in factors.items():
        out[name] = (out[name] * factor).astype(out[name].dtype)
    return out
```

```python
import concourse.bass as bass
from concourse import mybir
from contextlib import ExitStack

N_NODES = 12500
N_EDGES = 412500
P = 128
NB = 100
ROWS = NB * P
TI = 3224
LAST = N_EDGES - 127 * TI
PAD = 98 * P
GRP = 4
SB_GROUPS = 26
SB = GRP * SB_GROUPS
S_TURNS = TI // SB
HALF_G = SB_GROUPS // 2
HALF_T = SB // 2
NT = 3328
BODY = 32
HT = 16
TURNS = NT // BODY
F = 64
HID = 128


def gnn_kernel(nc, x, src, dst, ew, W1, b1, W2, b2, eW1, eb1, eW2, eb2, nW1, nb1, nW2, nb2, out):
    fp32 = mybir.dt.float32
    bf16 = mybir.dt.bfloat16
    i32 = mybir.dt.int32
    ALU = mybir.AluOpType
    ACT = mybir.ActivationFunctionType
    AX = mybir.AxisListType.X
    DS = bass.ds

    root = ExitStack()
    with root:
        def sem(name):
            return root.enter_context(nc.semaphore(name))

        s_mark = sem("s_mark")

        def wait_here(e, s, v):
            e.wait_ge(s, v)
            e.sem_inc(s_mark, 1)

        def sbt(ctx, name, shape, dt):
            return ctx.enter_context(nc.sbuf_tensor(name, shape, dt))

        def pst(ctx, name, dt=fp32):
            return ctx.enter_context(nc.psum_tensor(name, [P, 512 if dt == fp32 else 1024], dt))

        def dram(name, shape, dt):
            return nc.dram_tensor(name, shape, dt).ap()

        recs = {"d": dram("rec_d", (P * NT, 4), i32), "s": dram("rec_s", (P * NT, 4), i32)}
        tofs = {"d": dram("tof_d", (TURNS * 2, HT), i32), "s": dram("tof_s", (TURNS * 2, HT), i32)}
        tab_h = dram("tab_h", (ROWS, F), fp32)
        tab_e = dram("tab_e", (ROWS, F), fp32)
        tab_q = dram("tab_q", (ROWS, HID), fp32)

        X = sbt(root, "X", [P, NB, F], fp32)
        ACC = sbt(root, "ACC", [P, NB * HID], fp32)
        acc64 = ACC[:, 0:NB * F].rearrange("p (b f) -> p b f", f=F)
        Hn = ACC[:, NB * F:2 * NB * F].rearrange("p (b f) -> p b f", f=F)
        idn = sbt(root, "idn", [P, P], fp32)
        iota = sbt(root, "iota", [P, P], fp32)
        iotb = sbt(root, "iotb", [P, P], bf16)
        cinv = {"d": sbt(root, "cinv_d", [P, NB], fp32), "s": sbt(root, "cinv_s", [P, NB], fp32)}
        eps = sbt(root, "eps", [P, 1], fp32)

        s_ld = sem("s_ld")
        s_c = sem("s_c")
        s_pc = sem("s_pc")
        s_fill = sem("s_fill")

        st = ExitStack()
        with st:
            E = {"s": sbt(st, "E_s", [P, TI], i32), "d": sbt(st, "E_d", [P, TI], i32)}
            Wt = sbt(st, "Wt", [P, TI], fp32)
            HI = {k: sbt(st, f"HI_{k}", [P, TI], bf16) for k in "sd"}
            LO = {k: sbt(st, f"LO_{k}", [P, TI], bf16) for k in "sd"}
            U = sbt(st, "U", [P, P], bf16)
            ones = sbt(st, "ones", [P, P], bf16)
            zer = sbt(st, "zer", [P, 512], bf16)
            itmp = sbt(st, "itmp", [P, TI], i32)
            fill = sbt(st, "fill", [P, 416, 4], i32)
            oh = [sbt(st, f"oh{n}", [P, GRP, P], bf16) for n in range(2)]
            ol = [sbt(st, f"ol{n}", [P, GRP, P], bf16) for n in range(2)]
            tmp = sbt(st, "tmp", [P, GRP, P], fp32)
            junk = sbt(st, "junk", [P, P], fp32)
            pos = sbt(st, "pos", [P, SB], fp32)
            posi = sbt(st, "posi", [P, HALF_T], i32)
            sloti = sbt(st, "sloti", [P, HALF_T], i32)
            idx = [sbt(st, f"idx{n}", [P, HALF_T], i32) for n in range(2)]
            rec = [sbt(st, f"rec{n}", [P, HALF_T, 4], i32) for n in range(2)]
            scr = [sbt(st, f"scr{n}", [1, 16], i32) for n in range(2)]
            run = sbt(st, "run", [P, P], fp32)
            cnt = sbt(st, "cnt", [P, P], fp32)
            cnti = sbt(st, "cnti", [P, P], i32)
            zf = sbt(st, "zf", [P, P], fp32)
            R = [pst(st, f"R{n}") for n in range(2)]
            T = [pst(st, f"T{n}") for n in range(2)]
            C = pst(st, "C")
            Hh = pst(st, "Hh")

            with nc.Block() as block:
                @block.sync
                def _(e):
                    e.wait_ge(s_c, 3)
                    for t, a in ((E["s"], src), (E["d"], dst), (Wt, ew)):
                        e.dma_start(t[0:127, :], a[0:127 * TI].rearrange("(p t) -> p t", t=TI)).then_inc(s_ld, 16)
                        e.dma_start(t[127:128, 0:LAST], a[127 * TI:N_EDGES].rearrange("(a t) -> a t", a=1)).then_inc(s_ld, 16)
                    e.wait_ge(s_c, 4)
                    e.dma_start(X[:, 0:97, :], x[0:97 * P, :].rearrange("(b p) f -> p b f", p=P)).then_inc(s_ld, 16)
                    e.dma_start(X[0:N_NODES - 97 * P, 97, :], x[97 * P:N_NODES, :]).then_inc(s_ld, 16)
                    e.wait_ge(s_fill, 3)
                    for k in "ds":
                        v = recs[k].rearrange("(p t) c -> p t c", p=P)
                        for j in range(8):
                            e.dma_start(v[:, j * 416:(j + 1) * 416, :], fill[:, :, :]).then_inc(s_pc, 16)
                    e.wait_ge(s_ld, 128)
                    e.wait_ge(s_pc, 256)

                @block.vector
                def _(e):
                    e.memset(E["s"][:, :], PAD).then_inc(s_c, 1)
                    e.memset(E["d"][:, :], PAD).then_inc(s_c, 1)
                    e.memset(Wt[:, :], 0.0).then_inc(s_c, 1)
                    e.memset(X[:, :, :], 0.0).then_inc(s_c, 1)
                    e.memset(zer[:, :], 0.0)
                    e.memset(zf[:, :], 0.0)
                    e.memset(eps[:, :], 1e-5)
                    n = 4
                    e.wait_ge(s_ld, 128)
                    for k in "sd":
                        e.tensor_scalar(itmp[:, :], E[k][:, :], 7, None, ALU.arith_shift_right).then_inc(s_c, 1)
                        e.wait_ge(s_c, n + 1)
                        e.tensor_copy(HI[k][:, :], itmp[:, :]).then_inc(s_c, 1)
                        e.wait_ge(s_c, n + 2)
                        e.tensor_scalar(itmp[:, :], E[k][:, :], 127, None, ALU.bitwise_and).then_inc(s_c, 1)
                        e.wait_ge(s_c, n + 3)
                        e.tensor_copy(LO[k][:, :], itmp[:, :]).then_inc(s_c, 1)
                        e.wait_ge(s_c, n + 4)
                        n += 4

                @block.gpsimd
                def _(e):
                    e.iota(iota[:, :], pattern=[[1, P]], base=0, channel_multiplier=0,
                           allow_small_or_imprecise_dtypes=True).then_inc(s_fill, 1)
                    e.memset(fill[:, :, 1:3], 0).then_inc(s_fill, 1)
                    e.wait_ge(s_fill, 2)
                    e.memset(fill[:, :, 0:1], PAD)
                    e.memset(fill[:, :, 1:2].bitcast(fp32), -1.0)
                    e.memset(fill[:, :, 3:4], 98).then_inc(s_fill, 1)
                    e.wait_ge(s_fill, 3)
                    e.tensor_copy(iotb[:, :], iota[:, :]).then_inc(s_fill, 1)
                    e.memset(ones[:, :], 1.0).then_inc(s_fill, 1)
                    e.memset(idn[:, :], 0.0).then_inc(s_fill, 1)
                    e.memset(U[:, :], 1.0).then_inc(s_fill, 1)
                    e.wait_ge(s_fill, 7)
                    e.affine_select(out=U[:, :], in_=U[:, :], compare_op=ALU.is_gt, fill=0.0, base=0,
                                    pattern=[[1, P]], channel_multiplier=-1)
                    e.affine_select(out=idn[:, :], in_=idn[:, :], compare_op=ALU.not_equal, fill=1.0, base=0,
                                    pattern=[[-1, P]], channel_multiplier=1)

            def onehots(e, to, frm, i, g):
                v = frm[:, DS(i * SB + g * GRP, GRP)]
                return e.tensor_tensor(to[:, :, :], v.unsqueeze(2).to_broadcast([P, GRP, P]),
                                       iotb[:, :].unsqueeze(1).to_broadcast([P, GRP, P]), ALU.is_equal)

            for key, other in (("d", "s"), ("s", "d")):
                h_oh, h_pe, h_f = sem(f"h_oh{key}"), sem(f"h_pe{key}"), sem(f"h_f{key}")
                with nc.Block() as block:
                    @block.vector
                    def _(e):
                        e.sem_inc(h_pe, 2)
                        with e.Fori(0, S_TURNS) as i:
                            for g in range(SB_GROUPS):
                                e.wait_ge(h_pe, i * SB_GROUPS + g + 1)
                                onehots(e, oh[g % 2], HI[key], i, g).then_inc(h_oh, 1)
                        e.wait_ge(h_pe, 2 + S_TURNS * SB_GROUPS)
                        e.tensor_reduce(cnt[:, :], Hh[:, :].rearrange("p (g d) -> p d g", g=GRP), AX, ALU.add).then_inc(h_f, 1)
                        e.wait_ge(h_f, 1)
                        e.tensor_scalar(cnt[:, :], cnt[:, :], 127.0, None, ALU.add).then_inc(h_f, 1)
                        e.wait_ge(h_f, 2)
                        e.tensor_copy(cnti[:, :], cnt[:, :]).then_inc(h_f, 1)
                        e.wait_ge(h_f, 3)
                        e.tensor_scalar(cnti[:, :], cnti[:, :], 7, None, ALU.arith_shift_right).then_inc(h_f, 1)
                        e.wait_ge(h_f, 4)
                        e.tensor_copy(cnt[:, :], cnti[:, :]).then_inc(h_f, 1)
                        e.wait_ge(h_f, 5)
                        e.tensor_tensor_scan(run[:, :], cnt[:, :], zf[:, :], 0.0, ALU.add, ALU.add).then_inc(h_f, 1)
                        e.wait_ge(h_f, 6)
                        e.tensor_tensor(run[:, :], run[:, :], cnt[:, :], ALU.subtract).then_inc(h_f, 1)
                        e.wait_ge(h_f, 7)
                        e.tensor_scalar(run[:, :], run[:, :], 128.0, None, ALU.mult)

                    @block.tensor
                    def _(e):
                        e.matmul(Hh[:, :], lhsT=zer[:, 0:P], rhs=zer[:, :], start=True, stop=True)
                        e.matmul(C[:, 0:P], lhsT=zer[:, 0:P], rhs=zer[:, 0:P], start=True, stop=True)
                        with e.Fori(0, S_TURNS) as i:
                            for g in range(SB_GROUPS):
                                e.wait_ge(h_oh, i * SB_GROUPS + g + 1)
                                e.matmul(Hh[:, :], lhsT=ones[:, :], rhs=oh[g % 2][:, :, :].rearrange("p g d -> p (g d)"),
                                         start=False, stop=True, skip_group_check=True).then_inc(h_pe, 1)

                q_oh, q_r, q_v, q_i = sem(f"q_oh{key}"), sem(f"q_r{key}"), sem(f"q_v{key}"), sem(f"q_i{key}")
                q_s = [sem(f"q_s{key}{n}") for n in range(2)]
                NV = SB_GROUPS * 6 + 2 * 8
                with nc.Block() as block:
                    @block.vector
                    def _(e):
                        e.sem_inc(q_v, 1)
                        with e.Fori(0, S_TURNS) as i:
                            n = 0

                            def did(ins):
                                nonlocal n
                                ins.then_inc(q_v, 1)
                                n += 1
                                return n

                            def need(v):
                                e.wait_ge(q_v, i * NV + (v + 1))

                            for g in range(SB_GROUPS):
                                need(n)
                                if g == 0:
                                    e.wait_ge(q_r, i * SB_GROUPS + 1)
                                    onehots(e, oh[0], HI[key], i, 0)
                                    onehots(e, ol[0], LO[key], i, 0).then_inc(q_oh, 1)
                                if g + 1 < SB_GROUPS:
                                    e.wait_ge(q_r, i * SB_GROUPS + (g + 1))
                                    onehots(e, oh[(g + 1) % 2], HI[key], i, g + 1)
                                    onehots(e, ol[(g + 1) % 2], LO[key], i, g + 1).then_inc(q_oh, 1)
                                e.wait_ge(q_r, i * SB_GROUPS + (g + 2))
                                a = did(e.tensor_tensor(tmp[:, :, :], R[g % 2][:, :].rearrange("p (g d) -> p g d", g=GRP),
                                                        run[:, :].unsqueeze(1).to_broadcast([P, GRP, P]), ALU.add))
                                need(a)
                                for k in range(GRP):
                                    if k:
                                        need(n)
                                    did(e.tensor_tensor_reduce(out=junk[:, :], in0=tmp[:, k, :], in1=oh[g % 2][:, k, :],
                                                               scale=1.0, scalar=0.0, op0=ALU.mult, op1=ALU.add,
                                                               accum_out=pos[:, g * GRP + k:g * GRP + k + 1]))
                                did(e.tensor_tensor(run[:, :], run[:, :], T[g % 2][:, 0:P], ALU.add))
                                if g % HALF_G == HALF_G - 1:
                                    h = g // HALF_G
                                    t0 = i * SB + h * HALF_T
                                    need(n)
                                    e.wait_ge(q_s[h], i * (HALF_T * 16) + 16)
                                    a = did(e.tensor_copy(posi[:, :], pos[:, h * HALF_T:(h + 1) * HALF_T]))
                                    need(a)
                                    did(e.tensor_scalar(sloti[:, :], posi[:, :], 127, None, ALU.bitwise_and))
                                    a = did(e.tensor_scalar(posi[:, :], posi[:, :], 7, None, ALU.arith_shift_right))
                                    need(a)
                                    did(e.scalar_tensor_tensor(idx[h][:, :], sloti[:, :], float(NT), posi[:, :], ALU.mult, ALU.add))
                                    did(e.tensor_copy(rec[h][:, :, 0], E[other][:, DS(t0, HALF_T)]))
                                    did(e.tensor_copy(rec[h][:, :, 1].bitcast(fp32), LO[key][:, DS(t0, HALF_T)]))
                                    did(e.tensor_copy(rec[h][:, :, 2].bitcast(fp32), Wt[:, DS(t0, HALF_T)]))
                                    a = did(e.tensor_copy(rec[h][:, :, 3], HI[key][:, DS(t0, HALF_T)]))
                                    need(a)
                                    e.sem_inc(q_i, 1)
                            assert n == NV, n

                    @block.tensor
                    def _(e):
                        e.sem_inc(q_r, 1)
                        with e.Fori(0, S_TURNS) as i:
                            for g in range(SB_GROUPS):
                                b = g % 2
                                e.wait_ge(q_oh, i * SB_GROUPS + g + 1)
                                flat = oh[b][:, :, :].rearrange("p g d -> p (g d)")
                                e.matmul(R[b][:, :], lhsT=U[:, :], rhs=flat, start=True, stop=True)
                                for k in range(GRP - 1):
                                    m = GRP - 1 - k
                                    e.matmul(R[b][:, (k + 1) * P:], lhsT=ones[:, :],
                                             rhs=oh[b][:, k:k + 1, :].to_broadcast([P, m, P]), start=False, stop=True,
                                             skip_group_check=True)
                                for k in range(GRP):
                                    e.matmul(T[b][:, 0:P], lhsT=ones[:, :], rhs=oh[b][:, k, :], start=k == 0, stop=k == GRP - 1)
                                for k in range(GRP):
                                    last = e.matmul(C[:, 0:P], lhsT=ol[b][:, k, :], rhs=oh[b][:, k, :], start=False, stop=True,
                                                    skip_group_check=True)
                                last.then_inc(q_r, 1)

                    @block.gpsimd
                    def _(e):
                        for h in range(2):
                            e.dma_start(scr[h][:, :], src[0:16].rearrange("(a n) -> a n", a=1)).then_inc(q_s[h], 16)
                        with e.Fori(0, S_TURNS) as i:
                            for h in range(2):
                                wait_here(e, q_i, i * 2 + h + 1)
                                for t in range(HALF_T):
                                    e.indirect_dma_start(recs[key], bass.IndirectOffsetOnAxis(ap=idx[h][:, t:t + 1], axis=0),
                                                         rec[h][:, t, :], None).then_inc(q_s[h], 16)
                        for h in range(2):
                            e.wait_ge(q_s[h], S_TURNS * HALF_T * 16 + 16)

                z = sem(f"z_{key}")
                with nc.Block() as block:
                    @block.vector
                    def _(e):
                        e.tensor_scalar(cinv[key][:, :], C[:, 0:NB], 1.0, None, ALU.max).then_inc(z, 1)
                        e.wait_ge(z, 1)
                        e.reciprocal(cinv[key][:, :], cinv[key][:, :])

            z, zl = sem("z_t"), sem("z_l")
            tr = {k: sbt(st, f"tr_{k}", [TURNS, BODY, 4], i32) for k in "ds"}
            to = {k: sbt(st, f"to_{k}", [TURNS, BODY], i32) for k in "ds"}
            with nc.Block() as block:
                @block.sync
                def _(e):
                    for k in "ds":
                        e.dma_start(tr[k][:, :, :], recs[k][0:NT, :].rearrange("(a t) c -> a t c", t=BODY)).then_inc(zl, 16)
                    e.wait_ge(z, 2)
                    for k in "ds":
                        e.dma_start(tofs[k].rearrange("(a h) t -> a (h t)", h=2), to[k][:, :]).then_inc(zl, 16)
                    e.wait_ge(zl, 64)

                @block.vector
                def _(e):
                    e.wait_ge(zl, 32)
                    for k in "ds":
                        e.tensor_scalar(to[k][:, :], tr[k][:, :, 3], F, None, ALU.mult).then_inc(z, 1)

        def load_rows(name, a, n):
            t = sbt(root, name, [P, n], fp32)
            return t, a.rearrange("(a n) -> a n", a=1).to_broadcast([P, n])

        nW = {}
        loads = []
        for name, a, k, n in (("W1s", W1, F, F), ("W2s", W2, F, F), ("eW1a", eW1[0:F, :], F, HID), ("eW1b", eW1[F:2 * F, :], F, HID),
                              ("eW2s", eW2, HID, HID), ("nW1a", nW1[0:F, :], F, HID), ("nW1b", nW1[F:F + HID, :], HID, HID),
                              ("nW2s", nW2, HID, F)):
            nW[name] = sbt(root, name, [k, n], fp32)
            loads.append((nW[name][:, :], a))
        for name, a, n in (("b1s", b1, F), ("b2s", b2, F), ("nb2s", nb2, F), ("eb2s", eb2, HID),
                           ("w1b", eW1[2 * F:2 * F + 1, :].rearrange("a n -> (a n)"), HID)):
            nW[name], v = load_rows(name, a, n)
            loads.append((nW[name][:, :], v))
        for name, a in (("eb1s", eb1), ("nb1s", nb1)):
            nW[name] = sbt(root, name, [HID, 1], fp32)
            loads.append((nW[name][:, :], a.rearrange("(n a) -> n a", a=1)))

        sm = {n: sbt(root, f"ln_{n}", [P, NB], fp32) for n in ("m", "v")}
        s_n = sem("s_n")
        s_na = sem("s_na")
        s_w = sem("s_w")
        s_h0 = sem("s_h0")
        nn = [0]
        na = [0]

        def layernorm_relu(e, sq):
            def link(ins):
                nn[0] += 1
                ins.then_inc(s_n, 1)
                e.wait_ge(s_n, nn[0])

            link(e.tensor_reduce(sm["m"][:, :], X[:, :, :], AX, ALU.add))
            link(e.tensor_scalar(sm["m"][:, :], sm["m"][:, :], 1.0 / F, None, ALU.mult))
            link(e.tensor_tensor(Hn, X[:, :, :], sm["m"][:, :].unsqueeze(2).to_broadcast([P, NB, F]), ALU.subtract))
            link(e.tensor_tensor(sq, Hn, Hn, ALU.mult))
            link(e.tensor_reduce(sm["v"][:, :], sq, AX, ALU.add))
            e.wait_ge(s_na, na[0])
            link(e.reciprocal(sm["v"][:, :], sm["m"][:, :]))
            link(e.tensor_tensor(Hn, Hn, sm["v"][:, :].unsqueeze(2).to_broadcast([P, NB, F]), ALU.mult))
            link(e.tensor_scalar(Hn, Hn, 0.0, None, ALU.max))

        def ln_act(e, target):
            e.wait_ge(s_n, target)
            e.activation(sm["m"][:, :], sm["v"][:, :], ACT.Sqrt, bias=eps[:, 0:1], scale=1.0 / F).then_inc(s_na, 1)

        with nc.Block() as block:
            na[0] += 1

            @block.scalar
            def _(e):
                for o, a in loads:
                    e.dma_start(o, a).then_inc(s_w, 16)
                ln_act(e, 5)
                e.wait_ge(s_w, 16 * len(loads))

            @block.vector
            def _(e):
                layernorm_relu(e, acc64)

            @block.sync
            def _(e):
                e.wait_ge(s_n, 8)
                e.dma_start(tab_h.rearrange("(b p) f -> p b f", p=P), Hn).then_inc(s_h0, 16)
                e.wait_ge(s_h0, 16)

        s_rec = [sem(f"s_rec{h}") for h in range(2)]
        s_g = [sem(f"s_g{k}") for k in range(BODY)]
        s_oh, s_pe, s_add, s_pre = sem("s_oh"), sem("s_pe"), sem("s_add"), sem("s_pre")
        nhop = [0]

        def hop(table, k):
            r = nhop[0]
            nhop[0] += 1
            rv = recs[k].rearrange("(s t) c -> s t c", s=P)
            b_rec, b_g, b_oh, b_pe, b_add = r * TURNS * 32, r * TURNS * 16, r * TURNS * 2, r * TURNS * 4, r * (TURNS * BODY + 17)
            cx = ExitStack()
            with cx:
                G = sbt(cx, f"G{r}", [P, BODY, F], fp32)
                rb = [sbt(cx, f"rb{r}{h}", [P, HT, 4], i32) for h in range(2)]
                tb = [sbt(cx, f"tb{r}{h}", [1, HT], i32) for h in range(2)]
                O = [sbt(cx, f"O{r}{h}", [P, HT, P], fp32) for h in range(2)]
                ps = [pst(cx, f"ps{r}{b}") for b in range(4)]
                with nc.Block() as block:
                    @block.sync
                    def _(e):
                        with e.Fori(0, TURNS) as i:
                            for h in range(2):
                                e.wait_ge(s_add, i * BODY + (b_add + 1 + h * HT))
                                e.dma_start(rb[h][:, :, :], rv[:, DS(i * BODY + h * HT, HT), :]).then_inc(s_rec[h], 16)
                                e.dma_start(tb[h][:, :], tofs[k][DS(i * 2 + h, 1), :]).then_inc(s_rec[h], 16)

                    @block.gpsimd
                    def _(e):
                        with e.Fori(0, TURNS) as i:
                            for h in range(2):
                                wait_here(e, s_rec[h], i * 32 + (b_rec + 32))
                                for t in range(HT):
                                    s = h * HT + t
                                    e.indirect_dma_start(G[:, s, :], None, table,
                                                         bass.IndirectOffsetOnAxis(ap=rb[h][:, t, 0:1], axis=0)).then_inc(s_g[s], 16)

                    @block.tensor
                    def _(e):
                        with e.Fori(0, TURNS) as i:
                            for h in range(2):
                                e.wait_ge(s_oh, i * 2 + (b_oh + h + 1))
                                for t in range(HT):
                                    s = h * HT + t
                                    e.wait_ge(s_g[s], i * 16 + (b_g + 16))
                                    ins = e.matmul(ps[s // 8][:, (s % 8) * F:(s % 8 + 1) * F], lhsT=O[h][:, t, :], rhs=G[:, s, :],
                                                   start=True, stop=True)
                                    if s % 8 == 7:
                                        ins.then_inc(s_pe, 1)

                    @block.vector
                    def _(e):
                        e.memset(acc64, 0.0).then_inc(s_add, 17)
                        regs = [e.alloc_register(f"hr{r}_{n}") for n in range(HT)]
                        with e.Fori(0, TURNS) as i:
                            def onehot(h):
                                e.wait_ge(s_rec[h], i * 32 + (b_rec + 32))
                                e.tensor_tensor(O[h][:, :, :], rb[h][:, :, 1:2].bitcast(fp32).to_broadcast([P, HT, P]),
                                                iota[:, :].unsqueeze(1).to_broadcast([P, HT, P]), ALU.is_equal).then_inc(s_oh, 1)

                            onehot(0)
                            for h in range(2):
                                if h == 0:
                                    onehot(1)
                                e.load(regs, tb[h][0:1, :])
                                for t in range(HT):
                                    s = h * HT + t
                                    if s % 8 == 0:
                                        e.wait_ge(s_pe, i * 4 + (b_pe + s // 8 + 1))
                                    o = e.snap(regs[t], min_val=0, max_val=(NB - 1) * F)
                                    e.wait_ge(s_add, i * BODY + (b_add + 17 + s))
                                    e.tensor_tensor(ACC[:, DS(o, F)], ACC[:, DS(o, F)], ps[s // 8][:, (s % 8) * F:(s % 8 + 1) * F],
                                                    ALU.add).then_inc(s_add, 1)

        def scale_store(k, table):
            base = nn[0]
            w = nst[0]
            nst[0] += 16
            nn[0] += 1
            with nc.Block() as block:
                @block.vector
                def _(e):
                    e.tensor_tensor(Hn, acc64, cinv[k][:, :].unsqueeze(2).to_broadcast([P, NB, F]), ALU.mult).then_inc(s_n, 1)

                @block.sync
                def _(e):
                    e.wait_ge(s_n, base + 1)
                    e.dma_start(table.rearrange("(b p) f -> p b f", p=P), Hn).then_inc(s_w2, 16)
                    e.wait_ge(s_w2, w + 16)

        s_w2 = sem("s_w2")
        nst = [0]
        s_t, s_tc, s_m, s_o = sem("s_t"), sem("s_tc"), sem("s_m"), sem("s_o")
        GB = 4
        NG = NB // GB
        nlin = [0]

        def linear(name, w, finish):
            r = nlin[0]
            nlin[0] += 1
            b = r * NG
            cx = ExitStack()
            with cx:
                pt = [pst(cx, f"pt{name}{n}") for n in range(2)]
                po = [pst(cx, f"po{name}{n}") for n in range(2)]
                hT = [sbt(cx, f"hT{name}{n}", [F, GB, P], fp32) for n in range(2)]
                n = w.shape[1]
                with nc.Block() as block:
                    @block.tensor
                    def _(e):
                        for g in range(NG + 1):
                            if g < NG:
                                if g >= 2:
                                    e.wait_ge(s_tc, b + g - 1)
                                for j in range(GB):
                                    ins = e.transpose(pt[g % 2][0:F, j * P:(j + 1) * P], Hn[:, g * GB + j, :], idn[:, :])
                                ins.then_inc(s_t, 1)
                            if g >= 1:
                                q = g - 1
                                e.wait_ge(s_tc, b + q + 1)
                                if q >= 2:
                                    e.wait_ge(s_o, b + q - 1)
                                for j in range(GB):
                                    ins = e.matmul(po[q % 2][:, j * n:(j + 1) * n], lhsT=hT[q % 2][:, j, :], rhs=w[:, :], start=True, stop=True)
                                ins.then_inc(s_m, 1)

                    @block.scalar
                    def _(e):
                        for g in range(NG):
                            e.wait_ge(s_t, b + g + 1)
                            if g >= 2:
                                e.wait_ge(s_m, b + g - 1)
                            e.activation(hT[g % 2][:, :, :].rearrange("p j n -> p (j n)"), pt[g % 2][0:F, :], ACT.Copy).then_inc(s_tc, 1)

                    @block.vector
                    def _(e):
                        for g in range(NG):
                            e.wait_ge(s_m, b + g + 1)
                            finish(e, g, po[g % 2][:, 0:GB * n].rearrange("p (j n) -> p j n", n=n)).then_inc(s_o, 1)

        def bc(t, n):
            return t[:, :].unsqueeze(1).to_broadcast([P, GB, n])

        def store_block(table, v):
            w = nst[0]
            nst[0] += 16
            with nc.Block() as block:
                @block.sync
                def _(e):
                    e.dma_start(table.rearrange("(b p) f -> p b f", p=P), v).then_inc(s_w2, 16)
                    e.wait_ge(s_w2, w + 16)

        hop(tab_h, "d")
        scale_store("d", tab_e)
        hop(tab_e, "s")
        base = nn[0]
        nn[0] += 1
        with nc.Block() as block:
            @block.vector
            def _(e):
                e.tensor_tensor(Hn, acc64, cinv["s"][:, :].unsqueeze(2).to_broadcast([P, NB, F]), ALU.mult).then_inc(s_n, 1)
        linear("a", nW["W1s"], lambda e, g, p: e.tensor_tensor(acc64[:, g * GB:(g + 1) * GB, :], p, bc(nW["b1s"], F), ALU.add))
        base = nn[0]
        nn[0] += 1
        with nc.Block() as block:
            @block.vector
            def _(e):
                e.tensor_scalar(Hn, acc64, 0.0, None, ALU.max).then_inc(s_n, 1)
        store_block(tab_h, Hn)
        hop(tab_h, "d")
        scale_store("d", tab_e)
        hop(tab_e, "s")
        nn[0] += 1
        with nc.Block() as block:
            @block.vector
            def _(e):
                e.tensor_tensor(Hn, acc64, cinv["s"][:, :].unsqueeze(2).to_broadcast([P, NB, F]), ALU.mult).then_inc(s_n, 1)
        linear("b", nW["W2s"], lambda e, g, p: e.tensor_tensor(acc64[:, g * GB:(g + 1) * GB, :], p, bc(nW["b2s"], F), ALU.add))
        n0 = nn[0]
        nn[0] += 1
        with nc.Block() as block:
            na[0] += 1

            @block.scalar
            def _(e):
                ln_act(e, n0 + 6)

            @block.vector
            def _(e):
                e.tensor_tensor(X[:, :, :], X[:, :, :], acc64, ALU.add).then_inc(s_n, 1)
                e.wait_ge(s_n, n0 + 1)
                layernorm_relu(e, acc64)

        tab_n = dram("tab_n", (ROWS, F), fp32)
        store_block(tab_n, Hn)
        qx = ExitStack()
        with qx:
            Qt = sbt(qx, "Qt", [P, NB, HID], fp32)
            linear("q", nW["eW1b"], lambda e, g, p: e.tensor_copy(Qt[:, g * GB:(g + 1) * GB, :], p))
            store_block(tab_q, Qt[:, :, :])
        big = ExitStack()
        with big:
            P3 = sbt(big, "P3", [P, NB, 3, HID], bf16)
            px = ExitStack()
            with px:
                rem = [sbt(px, f"rem{n}", [P, GB, HID], fp32) for n in range(2)]
                s_sp = sem("s_sp")
                nsp = [0]

                def split(e, g, p):
                    def link(ins):
                        nsp[0] += 1
                        ins.then_inc(s_sp, 1)
                        e.wait_ge(s_sp, nsp[0])

                    bs = slice(g * GB, (g + 1) * GB)
                    link(e.tensor_copy(P3[:, bs, 0, :], p))
                    link(e.tensor_tensor(rem[0][:, :, :], p, P3[:, bs, 0, :], ALU.subtract))
                    link(e.tensor_copy(P3[:, bs, 1, :], rem[0][:, :, :]))
                    link(e.tensor_tensor(rem[1][:, :, :], rem[0][:, :, :], P3[:, bs, 1, :], ALU.subtract))
                    return e.tensor_copy(P3[:, bs, 2, :], rem[1][:, :, :])

                linear("p", nW["eW1a"], split)

            l_rec = [sem(f"l_rec{h}") for h in range(2)]
            l_oh, l_w, l_t, l_tc, l_p, l_y, l_2, l_zb, l_z, l_a, l_add = (
                sem(f"l_{n}") for n in ("oh", "w", "t", "tc", "p", "y", "2", "zb", "z", "a", "add"))
            b_g = nhop[0] * TURNS * 16
            rv = recs["s"].rearrange("(s t) c -> s t c", s=P)
            cx = ExitStack()
            with cx:
                G = sbt(cx, "GL", [P, BODY, HID], fp32)
                rb = [sbt(cx, f"rbL{h}", [P, HT, 4], i32) for h in range(2)]
                tb = [sbt(cx, f"tbL{h}", [1, HT], i32) for h in range(2)]
                O = [sbt(cx, f"OL{h}", [P, HT, P], fp32) for h in range(2)]
                ST = [sbt(cx, f"ST{n}", [P, 512], bf16) for n in range(2)]
                Y = sbt(cx, "Y", [P, 512], fp32)
                Zb = sbt(cx, "Zb", [P, 512], fp32)
                Z = sbt(cx, "Z", [P, 512], fp32)
                pT = [pst(cx, f"pT{n}") for n in range(2)]
                pP = [pst(cx, f"pP{n}") for n in range(2)]
                p2 = [pst(cx, f"p2{n}") for n in range(2)]
                pA = [pst(cx, f"pA{n}") for n in range(2)]
                Pf = P3[:, :, :, :].rearrange("p b c h -> p (b c h)")
                NGL = BODY // 4

                def done(e, s, i, g):
                    e.wait_ge(s, i * NGL + (g + 3))

                with nc.Block() as block:
                    @block.sync
                    def _(e):
                        with e.Fori(0, TURNS) as i:
                            for h in range(2):
                                e.wait_ge(l_add, i * BODY + (1 + h * HT))
                                e.dma_start(rb[h][:, :, :], rv[:, DS(i * BODY + h * HT, HT), :]).then_inc(l_rec[h], 16)
                                e.dma_start(tb[h][:, :], tofs["s"][DS(i * 2 + h, 1), :]).then_inc(l_rec[h], 16)

                    @block.gpsimd
                    def _(e):
                        with e.Fori(0, TURNS) as i:
                            for h in range(2):
                                wait_here(e, l_rec[h], i * 32 + 32)
                                for t in range(HT):
                                    s = h * HT + t
                                    e.indirect_dma_start(G[:, s, :], None, tab_q,
                                                         bass.IndirectOffsetOnAxis(ap=rb[h][:, t, 0:1], axis=0)).then_inc(s_g[s], 16)

                    @block.tensor
                    def _(e):
                        for s in (l_t, l_p, l_2, l_a):
                            e.sem_inc(s, 2)
                        regs = [e.alloc_register(f"lp_{n}") for n in range(HT)]
                        with e.Fori(0, TURNS) as i:
                            def stage_t(g):
                                if g % 4 == 0:
                                    e.wait_ge(l_oh, i * 2 + (g // 4 + 1))
                                done(e, l_tc, i, g - 2)
                                for j in range(4):
                                    ins = e.transpose(pT[g % 2][:, j * P:(j + 1) * P], O[g // 4][:, (g % 4) * 4 + j, :], idn[:, :])
                                ins.then_inc(l_t, 1)

                            def stage_p(g):
                                if g % 4 == 0:
                                    e.load(regs, tb[g // 4][0:1, :])
                                done(e, l_tc, i, g)
                                done(e, l_w, i, g)
                                done(e, l_y, i, g - 2)
                                for j in range(4):
                                    s = g * 4 + j
                                    o = e.snap(regs[(g % 4) * 4 + j], min_val=0, max_val=(NB - 1) * F)
                                    for c in range(3):
                                        e.matmul(pP[g % 2][:, j * P:(j + 1) * P], lhsT=Pf[:, DS(o * 6 + c * HID, HID)],
                                                 rhs=ST[g % 2][:, j * P:(j + 1) * P], start=c == 0, stop=False)
                                    ins = e.matmul(pP[g % 2][:, j * P:(j + 1) * P], lhsT=G[:, s, :], rhs=idn[:, :], start=False, stop=True)
                                ins.then_inc(l_p, 1)

                            def stage_2(g):
                                done(e, l_y, i, g)
                                done(e, l_zb, i, g - 2)
                                for j in range(4):
                                    ins = e.matmul(p2[g % 2][:, j * P:(j + 1) * P], lhsT=Y[:, j * P:(j + 1) * P], rhs=nW["eW2s"][:, :],
                                                   start=True, stop=True)
                                ins.then_inc(l_2, 1)

                            def stage_a(g):
                                done(e, l_z, i, g)
                                e.wait_ge(l_add, i * BODY + (17 + g * 4 - 4))
                                for j in range(4):
                                    ins = e.matmul(pA[g % 2][:, j * P:(j + 1) * P], lhsT=O[g // 4][:, (g % 4) * 4 + j, :],
                                                   rhs=Z[:, j * P:(j + 1) * P], start=True, stop=True)
                                ins.then_inc(l_a, 1)

                            for g in range(NGL + 3):
                                if g < NGL:
                                    stage_t(g)
                                if 1 <= g <= NGL:
                                    stage_p(g - 1)
                                if 2 <= g <= NGL + 1:
                                    stage_2(g - 2)
                                if 3 <= g:
                                    stage_a(g - 3)

                    @block.scalar
                    def _(e):
                        for s in (l_tc, l_y, l_z):
                            e.sem_inc(s, 2)
                        with e.Fori(0, TURNS) as i:
                            def copy_t(g):
                                done(e, l_t, i, g)
                                done(e, l_p, i, g - 2)
                                e.activation(ST[g % 2][:, :], pT[g % 2][:, :], ACT.Copy).then_inc(l_tc, 1)

                            for g in range(NGL + 2):
                                if g < NGL:
                                    copy_t(g)
                                if 1 <= g <= NGL:
                                    q = g - 1
                                    done(e, l_p, i, q)
                                    done(e, l_2, i, q - 1)
                                    e.activation(Y[:, :], pP[q % 2][:, :], ACT.Silu, bias=nW["eb1s"][:, 0:1]).then_inc(l_y, 1)
                                if 2 <= g:
                                    q = g - 2
                                    done(e, l_zb, i, q)
                                    done(e, l_a, i, q - 1)
                                    e.activation(Z[:, :], Zb[:, :], ACT.Silu).then_inc(l_z, 1)

                    @block.vector
                    def _(e):
                        e.memset(ACC[:, :], 0.0).then_inc(l_add, 17)
                        e.sem_inc(l_zb, 2)
                        e.sem_inc(l_w, 2)
                        regs = [e.alloc_register(f"la_{n}") for n in range(HT)]
                        with e.Fori(0, TURNS) as i:
                            def onehot(h):
                                e.wait_ge(l_rec[h], i * 32 + 32)
                                e.tensor_tensor(O[h][:, :, :], rb[h][:, :, 1:2].bitcast(fp32).to_broadcast([P, HT, P]),
                                                iota[:, :].unsqueeze(1).to_broadcast([P, HT, P]), ALU.is_equal).then_inc(l_oh, 1)

                            def weight(g):
                                for j in range(4):
                                    s = g * 4 + j
                                    e.wait_ge(s_g[s], i * 16 + (b_g + 16))
                                    ins = e.scalar_tensor_tensor(G[:, s, :], nW["w1b"][:, :], rb[s // HT][:, s % HT, 2:3].bitcast(fp32),
                                                                 G[:, s, :], ALU.mult, ALU.add)
                                ins.then_inc(l_w, 1)

                            def bias2(g):
                                done(e, l_2, i, g)
                                done(e, l_z, i, g - 1)
                                e.tensor_tensor(Zb[:, :].rearrange("p (j n) -> p j n", n=HID), p2[g % 2][:, :].rearrange("p (j n) -> p j n", n=HID),
                                                nW["eb2s"][:, :].unsqueeze(1).to_broadcast([P, 4, HID]), ALU.add).then_inc(l_zb, 1)

                            def add(g):
                                if g % 4 == 0:
                                    e.load(regs, tb[g // 4][0:1, :])
                                done(e, l_a, i, g)
                                for j in range(4):
                                    s = g * 4 + j
                                    o = e.snap(regs[s % HT], min_val=0, max_val=(NB - 1) * F)
                                    e.wait_ge(l_add, i * BODY + (17 + s))
                                    e.tensor_tensor(ACC[:, DS(o * 2, HID)], ACC[:, DS(o * 2, HID)], pA[g % 2][:, j * P:(j + 1) * P],
                                                    ALU.add).then_inc(l_add, 1)

                            for g in range(NGL + 3):
                                if g == 0:
                                    onehot(0)
                                if g < NGL:
                                    weight(g)
                                if g == 2:
                                    onehot(1)
                                if 2 <= g <= NGL + 1:
                                    bias2(g - 2)
                                if 3 <= g:
                                    add(g - 3)

        fx = ExitStack()
        with fx:
            H1 = sbt(fx, "H1", [P, NB, F], fp32)
            OUT = sbt(fx, "OUT", [P, NB, F], fp32)
            hT = [sbt(fx, f"fhT{n}", [F, 512], fp32) for n in range(2)]
            aT = [sbt(fx, f"faT{n}", [P, 512], fp32) for n in range(2)]
            u = [sbt(fx, f"fu{n}", [P, 512], fp32) for n in range(2)]
            ph = pst(fx, "ph")
            pa = pst(fx, "pa")
            pu = [pst(fx, f"pu{n}") for n in range(2)]
            po = [pst(fx, f"pof{n}") for n in range(2)]
            f_l, f_t, f_hc, f_ac, f_u, f_s, f_o, f_v, f_b = (sem(f"f_{n}") for n in ("l", "t", "hc", "ac", "u", "s", "o", "v", "b"))
            with nc.Block() as block:
                @block.sync
                def _(e):
                    e.dma_start(H1[:, :, :], tab_n.rearrange("(b p) f -> p b f", p=P)).then_inc(f_l, 16)
                    e.wait_ge(f_v, NG)
                    e.dma_start(out[0:97 * P, :].rearrange("(b p) f -> p b f", p=P), OUT[:, 0:97, :]).then_inc(f_l, 16)
                    e.dma_start(out[97 * P:N_NODES, :], OUT[0:N_NODES - 97 * P, 97, :]).then_inc(f_l, 16)
                    e.wait_ge(f_l, 48)

                @block.tensor
                def _(e):
                    e.wait_ge(f_l, 16)
                    for g in range(NG + 2):
                        if g < NG:
                            e.wait_ge(f_hc, g)
                            e.wait_ge(f_ac, g)
                            for j in range(GB):
                                e.transpose(ph[0:F, j * P:(j + 1) * P], H1[:, g * GB + j, :], idn[:, :])
                                ins = e.transpose(pa[:, j * P:(j + 1) * P], ACC[:, (g * GB + j) * HID:(g * GB + j + 1) * HID], idn[:, :])
                            ins.then_inc(f_t, 1)
                        if 1 <= g <= NG:
                            q = g - 1
                            e.wait_ge(f_hc, q + 1)
                            e.wait_ge(f_ac, q + 1)
                            if q >= 2:
                                e.wait_ge(f_s, q - 1)
                            e.matmul(pu[q % 2][:, :], lhsT=nW["nW1a"][:, :], rhs=hT[q % 2][:, :], start=True, stop=False)
                            e.matmul(pu[q % 2][:, :], lhsT=nW["nW1b"][:, :], rhs=aT[q % 2][:, :], start=False, stop=True).then_inc(f_u, 1)
                        if 2 <= g:
                            q = g - 2
                            e.wait_ge(f_s, q + 1)
                            if q >= 2:
                                e.wait_ge(f_v, q - 1)
                            for j in range(GB):
                                ins = e.matmul(po[q % 2][:, j * F:(j + 1) * F], lhsT=u[q % 2][:, j * P:(j + 1) * P], rhs=nW["nW2s"][:, :],
                                               start=True, stop=True)
                            ins.then_inc(f_o, 1)

                @block.scalar
                def _(e):
                    for g in range(NG + 1):
                        if g < NG:
                            e.wait_ge(f_t, g + 1)
                            if g >= 2:
                                e.wait_ge(f_u, g - 1)
                            e.activation(hT[g % 2][:, :], ph[0:F, :], ACT.Copy).then_inc(f_hc, 1)
                        if g >= 1:
                            q = g - 1
                            e.wait_ge(f_u, q + 1)
                            if q >= 2:
                                e.wait_ge(f_o, q - 1)
                            e.activation(u[q % 2][:, :], pu[q % 2][:, :], ACT.Silu, bias=nW["nb1s"][:, 0:1]).then_inc(f_s, 1)

                @block.vector
                def _(e):
                    for g in range(NG + 2):
                        if g < NG:
                            e.wait_ge(f_t, g + 1)
                            if g >= 2:
                                e.wait_ge(f_u, g - 1)
                            e.tensor_copy(aT[g % 2][:, :], pa[:, :]).then_inc(f_ac, 1)
                        if g >= 2:
                            q = g - 2
                            v = OUT[:, q * GB:(q + 1) * GB, :]
                            e.wait_ge(f_o, q + 1)
                            e.tensor_tensor(v, po[q % 2][:, 0:GB * F].rearrange("p (j n) -> p j n", n=F), bc(nW["nb2s"], F),
                                            ALU.add).then_inc(f_b, 1)
                            e.wait_ge(f_b, q + 1)
                            e.tensor_tensor(v, v, X[:, q * GB:(q + 1) * GB, :], ALU.add).then_inc(f_v, 1)


_INS = ['x', 'src', 'dst', 'edge_weight1', 'L0_gnn_W1', 'L0_gnn_b1', 'L0_gnn_W2', 'L0_gnn_b2', 'L1_gnn_eW1', 'L1_gnn_eb1',
        'L1_gnn_eW2', 'L1_gnn_eb2', 'L1_gnn_nW1', 'L1_gnn_nb1', 'L1_gnn_nW2', 'L1_gnn_nb2']


def kernel(**inputs):
    import numpy as np
    import concourse.bacc as bacc
    from concourse import mybir as mb
    from concourse.bass_utils import run_bass_kernel_spmd

    nc = bacc.Bacc("TRN2", target_bir_lowering=False, num_devices=1)
    arrays, args = {}, []
    for name in _INS:
        a = np.ascontiguousarray(inputs[name])
        if name == "edge_weight1":
            a = a.reshape(N_EDGES)
        arrays[f"in_{name}"] = a
        args.append(nc.dram_tensor(f"in_{name}", a.shape, mb.dt.from_np(a.dtype), kind="ExternalInput").ap())
    args.append(nc.dram_tensor("out_0", (N_NODES, F), mb.dt.float32, kind="ExternalOutput").ap())
    gnn_kernel(nc, *args)
    r = run_bass_kernel_spmd(nc, [arrays], core_ids=[0])
    return r.results[0]["out_0"]
```

```python
import concourse.bass as bass
from concourse import mybir
from contextlib import ExitStack

N_NODES = 12500
N_EDGES = 412500
P = 128
NB = 100
ROWS = NB * P
TI = 3224
LAST = N_EDGES - 127 * TI
PAD = 98 * P
GRP = 4
SB_GROUPS = 26
SB = GRP * SB_GROUPS
S_TURNS = TI // SB
EP = TI * P
ND = 99
HALF_G = SB_GROUPS // 2
HALF_T = SB // 2
NT = 3328
BODY = 32
HT = 16
TURNS = NT // BODY
NC = NT // P
F = 64
HID = 128


def gnn_kernel(nc, x, src, dst, ew, W1, b1, W2, b2, eW1, eb1, eW2, eb2, nW1, nb1, nW2, nb2, out):
    fp32 = mybir.dt.float32
    bf16 = mybir.dt.bfloat16
    i32 = mybir.dt.int32
    ALU = mybir.AluOpType
    ACT = mybir.ActivationFunctionType
    AX = mybir.AxisListType.X
    DS = bass.ds

    root = ExitStack()
    with root:
        def sem(name):
            return root.enter_context(nc.semaphore(name))

        s_mark = sem("s_mark")

        def wait_here(e, s, v):
            e.wait_ge(s, v)
            e.sem_inc(s_mark, 1)

        def sbt(ctx, name, shape, dt):
            return ctx.enter_context(nc.sbuf_tensor(name, shape, dt))

        def pst(ctx, name, dt=fp32):
            return ctx.enter_context(nc.psum_tensor(name, [P, 512 if dt == fp32 else 1024], dt))

        def dram(name, shape, dt):
            return nc.dram_tensor(name, shape, dt).ap()

        recs = {"d": dram("rec_d", (P * NT, 4), i32), "s": dram("rec_s", (P * NT, 4), i32)}
        tofs = {"d": dram("tof_d", (TURNS * 2, HT), i32), "s": dram("tof_s", (TURNS * 2, HT), i32)}
        recT = dram("rec_t", (NT, 2 * P), i32)
        SD = dram("pairs", (1, 2 * EP + 2 * P), i32)
        e0d = dram("e0d", (1, NT), i32)
        tab_h = dram("tab_h", (ROWS, F), fp32)
        tab_e = dram("tab_e", (ROWS, F), fp32)
        tab_q = dram("tab_q", (ROWS, HID), fp32)

        X = sbt(root, "X", [P, NB, F], fp32)
        ACC = sbt(root, "ACC", [P, NB * (2 * F + 1)], fp32)
        acc64 = ACC[:, 0:NB * F].rearrange("p (b f) -> p b f", f=F)
        acc65 = ACC[:, 0:NB * (F + 1)].rearrange("p (b f) -> p b f", f=F + 1)
        Hn = ACC[:, NB * (F + 1):NB * (2 * F + 1)].rearrange("p (b f) -> p b f", f=F)
        idn = sbt(root, "idn", [P, P], fp32)
        iota = sbt(root, "iota", [P, P], fp32)
        iotb = sbt(root, "iotb", [P, P], bf16)
        cinv = {"d": sbt(root, "cinv_d", [P, NB], fp32), "s": sbt(root, "cinv_s", [P, NB], fp32)}
        eps = sbt(root, "eps", [P, 1], fp32)

        s_ld, s_fill, s_c, s_pc = sem("s_ld"), sem("s_fill"), sem("s_c"), sem("s_pc")
        s_k, s_km = sem("s_k"), sem("s_km")
        st = ExitStack()
        with st:
            E = {"s": sbt(st, "E_s", [P, TI + 1], i32), "d": sbt(st, "E_d", [P, TI + 1], i32)}
            Wt = sbt(st, "Wt", [P, TI], fp32)
            HI = {k: sbt(st, f"HI_{k}", [P, TI], bf16) for k in "sd"}
            LO = {k: sbt(st, f"LO_{k}", [P, TI], bf16) for k in "sd"}
            pair = ACC[:, 0:2 * TI].bitcast(i32).rearrange("p (t c) -> p t c", c=2)
            itmp = ACC[:, 2 * TI:3 * TI].bitcast(i32)
            junkb = ACC[:, 3 * TI:3 * TI + TI // 2].bitcast(bf16)
            tail = sbt(st, "tail", [1, 2 * P], i32)
            U = sbt(st, "U", [P, P], bf16)
            ones = sbt(st, "ones", [P, P], bf16)
            onef = sbt(st, "onef", [P, P], fp32)
            fill = sbt(st, "fill", [P, 416, 4], i32)
            oh = [sbt(st, f"oh{n}", [P, GRP, P], bf16) for n in range(2)]
            tmp = sbt(st, "tmp", [P, GRP, P], fp32)
            junk = sbt(st, "junk", [P, P], fp32)
            pos = sbt(st, "pos", [P, SB], fp32)
            posi = sbt(st, "posi", [P, HALF_T], i32)
            sloti = sbt(st, "sloti", [P, HALF_T], i32)
            idx = [sbt(st, f"idx{n}", [P, HALF_T], i32) for n in range(2)]
            rec = [sbt(st, f"rec{n}", [P, HALF_T, 4], i32) for n in range(2)]
            scr = [sbt(st, f"scr{n}", [1, 16], i32) for n in range(2)]
            run = {k: sbt(st, f"run_{k}", [P, P], fp32) for k in "sd"}
            cum = {k: sbt(st, f"cum_{k}", [P, NB], fp32) for k in "sd"}
            Tt = sbt(st, "Tt", [P, NC], fp32)
            bT = {k: sbt(st, f"bT_{k}", [P, NC], fp32) for k in "sd"}
            e0 = sbt(st, "e0", [P, NC], fp32)
            c99 = {n: sbt(st, f"c99_{n}", [P, ND], fp32) for n in ("cnt", "nt", "tb", "st", "base", "delta", "z")}
            c99i = sbt(st, "c99i", [P, ND], i32)
            bad = sbt(st, "bad", [P, 1], fp32)
            badi = sbt(st, "badi", [P, 1], i32)
            rows = {n: sbt(st, f"rows_{n}", [NC, P], i32) for n in ("s", "d", "e")}
            e0s = [sbt(st, f"e0s{n}", [1, NT], i32) for n in range(2)]

            with nc.Block() as block:
                @block.sync
                def _(e):
                    e.wait_ge(s_c, 3)
                    for t, a in ((E["s"], src), (E["d"], dst), (Wt, ew)):
                        e.dma_start(t[0:127, 0:TI], a[0:127 * TI].rearrange("(p t) -> p t", t=TI)).then_inc(s_ld, 16)
                        e.dma_start(t[127:128, 0:LAST], a[127 * TI:N_EDGES].rearrange("(a t) -> a t", a=1)).then_inc(s_ld, 16)
                    with nc.allow_non_contiguous_dma(reason="127 elements"):
                        e.dma_start(E["d"][0:127, TI:TI + 1], dst[TI:].rearrange("(a n) -> a n", a=1)[0:1, 0:126 * TI + 1:TI].rearrange("a n -> n a")).then_inc(s_ld, 16)
                    e.wait_ge(s_c, 4)
                    e.dma_start(X[:, 0:97, :], x[0:97 * P, :].rearrange("(b p) f -> p b f", p=P)).then_inc(s_ld, 16)
                    e.dma_start(X[0:N_NODES - 97 * P, 97, :], x[97 * P:N_NODES, :]).then_inc(s_ld, 16)
                    e.wait_ge(s_fill, 3)
                    v = recs["s"].rearrange("(p t) c -> p t c", p=P)
                    for j in range(8):
                        e.dma_start(v[:, j * 416:(j + 1) * 416, :], fill[:, :, :]).then_inc(s_pc, 16)
                    e.wait_ge(s_c, 6)
                    e.dma_start(SD[0:1, 0:2 * EP].rearrange("a (p t) -> (a p) t", p=P), ACC[:, 0:2 * TI].bitcast(i32)).then_inc(s_pc, 16)
                    e.dma_start(SD[0:1, 2 * EP:2 * EP + 2 * P], tail[:, :]).then_inc(s_pc, 16)
                    e.wait_ge(s_ld, 144)
                    e.wait_ge(s_pc, 160)

                @block.vector
                def _(e):
                    e.memset(E["s"][:, :], PAD).then_inc(s_c, 1)
                    e.memset(E["d"][:, :], PAD).then_inc(s_c, 1)
                    e.memset(Wt[:, :], 0.0).then_inc(s_c, 1)
                    e.memset(X[:, :, :], 0.0).then_inc(s_c, 1)
                    e.memset(eps[:, :], 1e-5)
                    e.memset(c99["z"][:, :], 0.0)
                    e.memset(tail[:, :], PAD + P).then_inc(s_k, 1)
                    e.memset(rec[0][:, :, 3], 0)
                    e.memset(rec[1][:, :, 3], 0)
                    e.wait_ge(s_ld, 144)
                    e.tensor_copy(pair[:, :, 0], E["s"][:, 0:TI]).then_inc(s_c, 1)
                    e.tensor_copy(pair[:, :, 1], E["d"][:, 0:TI]).then_inc(s_c, 1)
                    n = 6
                    for k in "sd":
                        e.tensor_scalar(itmp, E[k][:, 0:TI], 7, None, ALU.arith_shift_right).then_inc(s_c, 1)
                        e.wait_ge(s_c, n + 1)
                        e.tensor_copy(HI[k][:, :], itmp).then_inc(s_c, 1)
                        e.wait_ge(s_c, n + 2)
                        e.tensor_scalar(itmp, E[k][:, 0:TI], 127, None, ALU.bitwise_and).then_inc(s_c, 1)
                        e.wait_ge(s_c, n + 3)
                        e.tensor_copy(LO[k][:, :], itmp).then_inc(s_c, 1)
                        e.wait_ge(s_c, n + 4)
                        n += 4

                @block.gpsimd
                def _(e):
                    e.iota(iota[:, :], pattern=[[1, P]], base=0, channel_multiplier=0,
                           allow_small_or_imprecise_dtypes=True).then_inc(s_fill, 1)
                    e.iota(Tt[:, :], pattern=[[P, NC]], base=0, channel_multiplier=1, allow_small_or_imprecise_dtypes=True)
                    e.memset(fill[:, :, 1:4], 0).then_inc(s_fill, 1)
                    e.wait_ge(s_fill, 2)
                    e.memset(fill[:, :, 0:1], PAD)
                    e.memset(fill[:, :, 1:2].bitcast(fp32), -1.0).then_inc(s_fill, 1)
                    e.wait_ge(s_fill, 3)
                    e.tensor_copy(iotb[:, :], iota[:, :]).then_inc(s_fill, 1)
                    e.memset(ones[:, :], 1.0).then_inc(s_fill, 1)
                    e.memset(onef[:, :], 1.0)
                    e.memset(idn[:, :], 0.0).then_inc(s_fill, 1)
                    e.memset(U[:, :], 1.0).then_inc(s_fill, 1)
                    e.wait_ge(s_fill, 7)
                    e.affine_select(out=U[:, :], in_=U[:, :], compare_op=ALU.is_gt, fill=0.0, base=0,
                                    pattern=[[1, P]], channel_multiplier=-1)
                    e.affine_select(out=idn[:, :], in_=idn[:, :], compare_op=ALU.not_equal, fill=1.0, base=0,
                                    pattern=[[-1, P]], channel_multiplier=1)

            kx = ExitStack()
            with kx:
                ge, gd = (ACC[:, n * NC * ND:(n + 1) * NC * ND].rearrange("p (c b) -> p c b", b=ND) for n in range(2))
                pk = pst(kx, "pk")
                pr = pst(kx, "pr")
                kn = [1]
                with nc.Block() as block:
                    @block.vector
                    def _(e):
                        def link(ins):
                            kn[0] += 1
                            ins.then_inc(s_k, 1)
                            e.wait_ge(s_k, kn[0])

                        def clear(k):
                            e.memset(cum[k][:, 0:1], float(TI))
                            link(e.memset(cum[k][:, ND:NB], 0.0))

                        for k in "sd":
                            clear(k)
                        link(e.tensor_tensor(itmp, E["d"][:, 1:TI + 1], E["d"][:, 0:TI], ALU.is_lt))
                        link(e.tensor_reduce(bad[:, :], itmp, AX, ALU.max))
                        for k in "sd":
                            for b in range(1, ND):
                                link(e.tensor_scalar(junkb, HI[k][:, :], float(b), 0.0, ALU.is_ge, ALU.add, accum_out=cum[k][:, b:b + 1]))
                        e.sem_inc(s_km, 1)
                        e.wait_ge(s_km, 2)
                        for k in "ds":
                            tot = pk[:, 0:NB] if k == "d" else pk[:, 128:128 + NB]
                            c = c99
                            link(e.tensor_copy(cum[k][:, :], tot))
                            link(e.tensor_tensor(c["cnt"][:, :], cum[k][:, 0:ND], cum[k][:, 1:NB], ALU.subtract))
                            link(e.tensor_scalar(c["cnt"][:, :], c["cnt"][:, :], 127.0, None, ALU.add))
                            link(e.tensor_copy(c99i[:, :], c["cnt"][:, :]))
                            link(e.tensor_scalar(c99i[:, :], c99i[:, :], 7, None, ALU.arith_shift_right))
                            link(e.tensor_copy(c["nt"][:, :], c99i[:, :]))
                            link(e.tensor_tensor_scan(c["tb"][:, :], c["nt"][:, :], c["z"][:, :], 0.0, ALU.add, ALU.add))
                            link(e.tensor_tensor(c["tb"][:, :], c["tb"][:, :], c["nt"][:, :], ALU.subtract))
                            link(e.memset(run[k][:, :], 0.0))
                            link(e.tensor_scalar(run[k][:, 0:ND], c["tb"][:, :], 128.0, None, ALU.mult))
                            link(e.tensor_tensor(ge[:, :, :], Tt[:, :].unsqueeze(2).to_broadcast([P, NC, ND]),
                                                 c["tb"][:, :].unsqueeze(1).to_broadcast([P, NC, ND]), ALU.is_ge))
                            link(e.tensor_reduce(bT[k][:, :], ge[:, :, :], AX, ALU.add))
                            link(e.tensor_scalar(bT[k][:, :], bT[k][:, :], -1.0, None, ALU.add))
                            if k == "d":
                                link(e.scalar_tensor_tensor(c["st"][:, :], cum[k][:, 0:ND], -1.0,
                                                            cum[k][:, 0:1].to_broadcast([P, ND]), ALU.mult, ALU.add))
                                link(e.tensor_tensor(c["base"][:, :], c["st"][:, :], run[k][:, 0:ND], ALU.subtract))
                                link(e.tensor_copy(c["delta"][:, :], c["base"][:, :]))
                                link(e.tensor_tensor(c["delta"][:, 1:ND], c["base"][:, 1:ND], c["base"][:, 0:ND - 1], ALU.subtract))
                                link(e.tensor_tensor(gd[:, :, :], ge[:, :, :], c["delta"][:, :].unsqueeze(1).to_broadcast([P, NC, ND]),
                                                     ALU.mult))
                                link(e.tensor_reduce(e0[:, :], gd[:, :, :], AX, ALU.add))
                                link(e.scalar_tensor_tensor(e0[:, :], Tt[:, :], 128.0, e0[:, :], ALU.mult, ALU.add))
                                link(e.tensor_scalar(e0[:, :], e0[:, :], float(EP), 0.0, ALU.min, ALU.max))
                                link(e.tensor_scalar(badi[:, 0:1], pk[:, 256:257], 0.5, None, ALU.is_ge))
                        e.sem_inc(s_km, 1)
                        e.wait_ge(s_km, 4)
                        for n, k in enumerate("sde"):
                            link(e.tensor_copy(rows[k][:, :], pr[0:NC, n * P:(n + 1) * P]))

                    @block.tensor
                    def _(e):
                        e.wait_ge(s_km, 1)
                        e.matmul(pk[:, 0:NB], lhsT=onef[:, :], rhs=cum["d"][:, :], start=True, stop=True)
                        e.matmul(pk[:, 256:257], lhsT=onef[:, :], rhs=bad[:, :], start=True, stop=True)
                        e.matmul(pk[:, 128:128 + NB], lhsT=onef[:, :], rhs=cum["s"][:, :], start=True, stop=True).then_inc(s_km, 1)
                        e.wait_ge(s_km, 3)
                        e.transpose(pr[0:NC, 0:P], bT["s"][:, :], idn[:, :])
                        e.transpose(pr[0:NC, P:2 * P], bT["d"][:, :], idn[:, :])
                        e.transpose(pr[0:NC, 2 * P:3 * P], e0[:, :], idn[:, :]).then_inc(s_km, 1)
                z0 = sem("z0")
                with nc.Block() as block:
                    @block.sync
                    def _(e):
                        for k in "sd":
                            e.dma_start(tofs[k].rearrange("(c a) t -> c (a t)", c=NC), rows[k][:, :]).then_inc(z0, 16)
                        e.dma_start(e0d.rearrange("a (c t) -> (a c) t", c=NC), rows["e"][:, :]).then_inc(z0, 16)
                        e.wait_ge(z0, 48)
                        for n in range(2):
                            e.dma_start(e0s[n][:, :], e0d).then_inc(z0, 16)
                        e.wait_ge(z0, 80)

            def onehots(e, to, frm, i, g):
                v = frm[:, DS(i * SB + g * GRP, GRP)]
                return e.tensor_tensor(to[:, :, :], v.unsqueeze(2).to_broadcast([P, GRP, P]),
                                       iotb[:, :].unsqueeze(1).to_broadcast([P, GRP, P]), ALU.is_equal)

            def sort(key, other, guard=None, beside=None):
                def guarded(body):
                    def program(e):
                        if guard is None:
                            body(e)
                        else:
                            with e.If(guard(e)):
                                body(e)
                    return program

                q_oh, q_r, q_v, q_i = sem(f"q_oh{key}"), sem(f"q_r{key}"), sem(f"q_v{key}"), sem(f"q_i{key}")
                q_s = [sem(f"q_s{key}{n}") for n in range(2)]
                NV = SB_GROUPS * 6 + 2 * 7
                px = ExitStack()
                with px:
                    R = [pst(px, f"R{key}{n}") for n in range(2)]
                    T = [pst(px, f"T{key}{n}") for n in range(2)]
                    rn = run[key]
                    with nc.Block() as block:
                        @block.vector
                        @guarded
                        def _(e):
                            e.sem_inc(q_v, 1)
                            with e.Fori(0, S_TURNS) as i:
                                n = 0

                                def did(ins):
                                    nonlocal n
                                    ins.then_inc(q_v, 1)
                                    n += 1
                                    return n

                                def need(v):
                                    e.wait_ge(q_v, i * NV + (v + 1))

                                for g in range(SB_GROUPS):
                                    need(n)
                                    if g == 0:
                                        e.wait_ge(q_r, i * SB_GROUPS + 1)
                                        onehots(e, oh[0], HI[key], i, 0).then_inc(q_oh, 1)
                                    if g + 1 < SB_GROUPS:
                                        e.wait_ge(q_r, i * SB_GROUPS + (g + 1))
                                        onehots(e, oh[(g + 1) % 2], HI[key], i, g + 1).then_inc(q_oh, 1)
                                    e.wait_ge(q_r, i * SB_GROUPS + (g + 2))
                                    a = did(e.tensor_tensor(tmp[:, :, :], R[g % 2][:, :].rearrange("p (g d) -> p g d", g=GRP),
                                                            rn[:, :].unsqueeze(1).to_broadcast([P, GRP, P]), ALU.add))
                                    need(a)
                                    for k in range(GRP):
                                        if k:
                                            need(n)
                                        did(e.tensor_tensor_reduce(out=junk[:, :], in0=tmp[:, k, :], in1=oh[g % 2][:, k, :],
                                                                   scale=1.0, scalar=0.0, op0=ALU.mult, op1=ALU.add,
                                                                   accum_out=pos[:, g * GRP + k:g * GRP + k + 1]))
                                    did(e.tensor_tensor(rn[:, :], rn[:, :], T[g % 2][:, 0:P], ALU.add))
                                    if g % HALF_G == HALF_G - 1:
                                        h = g // HALF_G
                                        t0 = i * SB + h * HALF_T
                                        need(n)
                                        e.wait_ge(q_s[h], i * (HALF_T * 16) + 16)
                                        a = did(e.tensor_copy(posi[:, :], pos[:, h * HALF_T:(h + 1) * HALF_T]))
                                        need(a)
                                        did(e.tensor_scalar(sloti[:, :], posi[:, :], 127, None, ALU.bitwise_and))
                                        a = did(e.tensor_scalar(posi[:, :], posi[:, :], 7, None, ALU.arith_shift_right))
                                        need(a)
                                        did(e.scalar_tensor_tensor(idx[h][:, :], sloti[:, :], float(NT), posi[:, :], ALU.mult, ALU.add))
                                        did(e.tensor_copy(rec[h][:, :, 0], E[other][:, DS(t0, HALF_T)]))
                                        did(e.tensor_copy(rec[h][:, :, 1].bitcast(fp32), LO[key][:, DS(t0, HALF_T)]))
                                        a = did(e.tensor_copy(rec[h][:, :, 2].bitcast(fp32), Wt[:, DS(t0, HALF_T)]))
                                        need(a)
                                        e.sem_inc(q_i, 1)
                                assert n == NV, n

                        @block.tensor
                        @guarded
                        def _(e):
                            e.sem_inc(q_r, 1)
                            with e.Fori(0, S_TURNS) as i:
                                for g in range(SB_GROUPS):
                                    b = g % 2
                                    e.wait_ge(q_oh, i * SB_GROUPS + g + 1)
                                    flat = oh[b][:, :, :].rearrange("p g d -> p (g d)")
                                    e.matmul(R[b][:, :], lhsT=U[:, :], rhs=flat, start=True, stop=True)
                                    for k in range(GRP - 1):
                                        m = GRP - 1 - k
                                        e.matmul(R[b][:, (k + 1) * P:], lhsT=ones[:, :],
                                                 rhs=oh[b][:, k:k + 1, :].to_broadcast([P, m, P]), start=False, stop=True,
                                                 skip_group_check=True)
                                    for k in range(GRP):
                                        last = e.matmul(T[b][:, 0:P], lhsT=ones[:, :], rhs=oh[b][:, k, :], start=k == 0, stop=k == GRP - 1)
                                    last.then_inc(q_r, 1)

                        @block.gpsimd
                        @guarded
                        def _(e):
                            for h in range(2):
                                e.dma_start(scr[h][:, :], src[0:16].rearrange("(a n) -> a n", a=1)).then_inc(q_s[h], 16)
                            with e.Fori(0, S_TURNS) as i:
                                for h in range(2):
                                    wait_here(e, q_i, i * 2 + h + 1)
                                    for t in range(HALF_T):
                                        e.indirect_dma_start(recs[key], bass.IndirectOffsetOnAxis(ap=idx[h][:, t:t + 1], axis=0),
                                                             rec[h][:, t, :], None).then_inc(q_s[h], 16)
                            for h in range(2):
                                e.wait_ge(q_s[h], S_TURNS * HALF_T * 16 + 16)

                        if beside:
                            beside(block)

            z1 = [sem(f"z1{h}") for h in range(2)]

            def runs(block):
                def half(e, h):
                    regs = [e.alloc_register(f"rr{h}_{n}") for n in range(HT)]
                    with e.Fori(0, TURNS) as i:
                        e.load(regs, e0s[h][0:1, DS(i * BODY + h * HT, HT)])
                        for t in range(HT):
                            o = e.snap(regs[t], min_val=0, max_val=EP)
                            e.dma_start(recT[DS(i * BODY + (h * HT + t), 1), :], SD[0:1, DS(o * 2, 2 * P)]).then_inc(z1[h], 16)
                    e.wait_ge(z1[h], NT // 2 * 16)

                block.sync(lambda e: half(e, 0))
                block.scalar(lambda e: half(e, 1))

            sort("s", "d", None, runs)

            tx = ExitStack()
            with tx:
                TR = [sbt(tx, f"TR{n}", [P, P, 2], i32) for n in range(2)]
                TF = [sbt(tx, f"TF{n}", [P, 2, P], fp32) for n in range(2)]
                RD = [sbt(tx, f"RD{n}", [P, P, 4], i32) for n in range(2)]
                b128 = sbt(tx, "b128", [P, NC], fp32)
                pq = [pst(tx, f"pq{n}") for n in range(2)]
                t_l, t_f, t_p, t_r, t_s = sem("t_l0"), sem("t_f"), sem("t_p"), sem("t_r"), [sem("t_s0"), sem("t_s1")]
                t_l = [t_l, sem("t_l1")]
                rv = recs["d"].rearrange("(s t) c -> s t c", s=P)
                with nc.Block() as block:
                    @block.sync
                    def _(e):
                        for c in range(NC + 1):
                            if c < NC:
                                if c >= 2:
                                    e.wait_ge(t_f, c)
                                e.dma_start(TR[c % 2][:, :, :], recT[c * P:(c + 1) * P, :].rearrange("t (s c) -> t s c", c=2)).then_inc(t_l[c % 2], 16)
                            if c >= 1:
                                q = c - 1
                                e.wait_ge(t_r, 2 * q + 4)
                                e.dma_start(rv[:, q * P:(q + 1) * P, :], RD[q % 2][:, :, :]).then_inc(t_s[q % 2], 16)
                        for h in range(2):
                            e.wait_ge(t_s[h], NC // 2 * 16)

                    @block.vector
                    def _(e):
                        e.memset(RD[0][:, :, :], 0).then_inc(t_r, 1)
                        e.memset(RD[1][:, :, :], 0).then_inc(t_r, 1)
                        e.wait_ge(t_r, 2)
                        e.tensor_scalar(b128[:, :], bT["d"][:, :], 128.0, None, ALU.mult).then_inc(t_f, 1)
                        e.wait_ge(t_f, 1)
                        for c in range(NC + 1):
                            if c < NC:
                                e.wait_ge(t_l[c % 2], (c // 2 + 1) * 16)
                                if c >= 2:
                                    e.wait_ge(t_p, c - 1)
                                e.tensor_copy(TF[c % 2][:, 0, :], TR[c % 2][:, :, 0])
                                e.tensor_scalar(TF[c % 2][:, 1, :], TR[c % 2][:, :, 1], b128[:, c:c + 1], None, ALU.subtract).then_inc(t_f, 1)
                            if c >= 1:
                                q = c - 1
                                e.wait_ge(t_p, q + 1)
                                if q >= 2:
                                    e.wait_ge(t_s[q % 2], (q // 2) * 16)
                                e.tensor_copy(RD[q % 2][:, :, 0], pq[q % 2][:, 0:P]).then_inc(t_r, 1)
                                e.tensor_copy(RD[q % 2][:, :, 1].bitcast(fp32), pq[q % 2][:, P:2 * P]).then_inc(t_r, 1)

                    @block.tensor
                    def _(e):
                        for c in range(NC):
                            e.wait_ge(t_f, c + 2)
                            if c >= 2:
                                e.wait_ge(t_r, 2 * (c - 2) + 4)
                            e.transpose(pq[c % 2][:, 0:P], TF[c % 2][:, 0, :], idn[:, :])
                            e.transpose(pq[c % 2][:, P:2 * P], TF[c % 2][:, 1, :], idn[:, :]).then_inc(t_p, 1)

            z2 = sem("z2")

            def general(e):
                return e.value_load(badi[0:1, 0:1], min_val=0, max_val=1)

            with nc.Block() as block:
                @block.sync
                def _(e):
                    with e.If(general(e)):
                        v = recs["d"].rearrange("(p t) c -> p t c", p=P)
                        for j in range(8):
                            e.dma_start(v[:, j * 416:(j + 1) * 416, :], fill[:, :, :]).then_inc(z2, 16)
                        e.wait_ge(z2, 128)
            sort("d", "s", general)

        def load_rows(name, a, n):
            t = sbt(root, name, [P, n], fp32)
            return t, a.rearrange("(a n) -> a n", a=1).to_broadcast([P, n])

        nW = {}
        loads = []
        for name, a, k, n in (("W1s", W1, F, F), ("W2s", W2, F, F), ("eW1a", eW1[0:F, :], F, HID), ("eW1b", eW1[F:2 * F, :], F, HID),
                              ("eW2s", eW2, HID, HID), ("nW1a", nW1[0:F, :], F, HID), ("nW1b", nW1[F:F + HID, :], HID, HID),
                              ("nW2s", nW2, HID, F)):
            nW[name] = sbt(root, name, [k, n], fp32)
            loads.append((nW[name][:, :], a))
        for name, a, n in (("b1s", b1, F), ("b2s", b2, F), ("nb2s", nb2, F), ("eb2s", eb2, HID),
                           ("w1b", eW1[2 * F:2 * F + 1, :].rearrange("a n -> (a n)"), HID)):
            nW[name], v = load_rows(name, a, n)
            loads.append((nW[name][:, :], v))
        for name, a in (("eb1s", eb1), ("nb1s", nb1)):
            nW[name] = sbt(root, name, [HID, 1], fp32)
            loads.append((nW[name][:, :], a.rearrange("(n a) -> n a", a=1)))

        sm = {n: sbt(root, f"ln_{n}", [P, NB], fp32) for n in ("m", "v")}
        s_n = sem("s_n")
        s_na = sem("s_na")
        s_w = sem("s_w")
        s_h0 = sem("s_h0")
        nn = [0]
        na = [0]

        def layernorm_relu(e, sq):
            def link(ins):
                nn[0] += 1
                ins.then_inc(s_n, 1)
                e.wait_ge(s_n, nn[0])

            link(e.tensor_reduce(sm["m"][:, :], X[:, :, :], AX, ALU.add))
            link(e.tensor_scalar(sm["m"][:, :], sm["m"][:, :], 1.0 / F, None, ALU.mult))
            link(e.tensor_tensor(Hn, X[:, :, :], sm["m"][:, :].unsqueeze(2).to_broadcast([P, NB, F]), ALU.subtract))
            link(e.tensor_tensor(sq, Hn, Hn, ALU.mult))
            link(e.tensor_reduce(sm["v"][:, :], sq, AX, ALU.add))
            e.wait_ge(s_na, na[0])
            link(e.reciprocal(sm["v"][:, :], sm["m"][:, :]))
            link(e.tensor_tensor(Hn, Hn, sm["v"][:, :].unsqueeze(2).to_broadcast([P, NB, F]), ALU.mult))
            link(e.tensor_scalar(Hn, Hn, 0.0, None, ALU.max))

        def ln_act(e, target):
            e.wait_ge(s_n, target)
            e.activation(sm["m"][:, :], sm["v"][:, :], ACT.Sqrt, bias=eps[:, 0:1], scale=1.0 / F).then_inc(s_na, 1)

        with nc.Block() as block:
            na[0] += 1

            @block.scalar
            def _(e):
                for o, a in loads:
                    e.dma_start(o, a).then_inc(s_w, 16)
                ln_act(e, 5)
                e.wait_ge(s_w, 16 * len(loads))

            @block.vector
            def _(e):
                layernorm_relu(e, acc64)

            @block.sync
            def _(e):
                e.wait_ge(s_n, 8)
                e.dma_start(tab_h.rearrange("(b p) f -> p b f", p=P), Hn).then_inc(s_h0, 16)
                e.wait_ge(s_h0, 16)

        s_rec = [sem(f"s_rec{h}") for h in range(2)]
        s_g = [sem(f"s_g{k}") for k in range(BODY)]
        s_oh, s_pe, s_add, s_pre = sem("s_oh"), sem("s_pe"), sem("s_add"), sem("s_pre")
        nhop = [0]

        def hop(table, k, count=False):
            W = F + 1 if count else F
            r = nhop[0]
            nhop[0] += 1
            rv = recs[k].rearrange("(s t) c -> s t c", s=P)
            b_rec, b_g, b_oh, b_pe, b_add = r * TURNS * 32, r * TURNS * 16, r * TURNS * 2, r * TURNS * 8, r * (TURNS * BODY + 17)
            cx = ExitStack()
            with cx:
                G = sbt(cx, f"G{r}", [P, BODY, W], fp32)
                rb = [sbt(cx, f"rb{r}{h}", [P, HT, 4], i32) for h in range(2)]
                tb = [sbt(cx, f"tb{r}{h}", [1, HT], i32) for h in range(2)]
                O = [sbt(cx, f"O{r}{h}", [P, HT, P], fp32) for h in range(2)]
                ps = [pst(cx, f"ps{r}{b}") for b in range(8)]
                with nc.Block() as block:
                    @block.sync
                    def _(e):
                        with e.Fori(0, TURNS) as i:
                            for h in range(2):
                                e.wait_ge(s_add, i * BODY + (b_add + 1 + h * HT))
                                e.dma_start(rb[h][:, :, :], rv[:, DS(i * BODY + h * HT, HT), :]).then_inc(s_rec[h], 16)
                                e.dma_start(tb[h][:, :], tofs[k][DS(i * 2 + h, 1), :]).then_inc(s_rec[h], 16)

                    @block.gpsimd
                    def _(e):
                        with e.Fori(0, TURNS) as i:
                            for h in range(2):
                                wait_here(e, s_rec[h], i * 32 + (b_rec + 32))
                                for t in range(HT):
                                    s = h * HT + t
                                    e.indirect_dma_start(G[:, s, 0:F], None, table,
                                                         bass.IndirectOffsetOnAxis(ap=rb[h][:, t, 0:1], axis=0)).then_inc(s_g[s], 16)

                    @block.tensor
                    def _(e):
                        with e.Fori(0, TURNS) as i:
                            for h in range(2):
                                e.wait_ge(s_oh, i * 2 + (b_oh + h + 1))
                                for t in range(HT):
                                    s = h * HT + t
                                    e.wait_ge(s_g[s], i * 16 + (b_g + 16))
                                    ins = e.matmul(ps[s // 4][:, (s % 4) * W:(s % 4 + 1) * W], lhsT=O[h][:, t, :], rhs=G[:, s, :],
                                                   start=True, stop=True)
                                    if s % 4 == 3:
                                        ins.then_inc(s_pe, 1)

                    @block.vector
                    def _(e):
                        e.memset(ACC[:, 0:NB * W], 0.0).then_inc(s_add, 17)
                        if count:
                            e.memset(G[:, :, F:W], 1.0)
                        regs = [e.alloc_register(f"hr{r}_{n}") for n in range(HT)]
                        with e.Fori(0, TURNS) as i:
                            def onehot(h):
                                e.wait_ge(s_rec[h], i * 32 + (b_rec + 32))
                                e.tensor_tensor(O[h][:, :, :], rb[h][:, :, 1:2].bitcast(fp32).to_broadcast([P, HT, P]),
                                                iota[:, :].unsqueeze(1).to_broadcast([P, HT, P]), ALU.is_equal).then_inc(s_oh, 1)

                            onehot(0)
                            for h in range(2):
                                if h == 0:
                                    onehot(1)
                                e.load(regs, tb[h][0:1, :])
                                for t in range(HT):
                                    s = h * HT + t
                                    if s % 4 == 0:
                                        e.wait_ge(s_pe, i * 8 + (b_pe + s // 4 + 1))
                                    o = e.snap(regs[t], min_val=0, max_val=NB - 1)
                                    e.wait_ge(s_add, i * BODY + (b_add + 17 + s))
                                    e.tensor_tensor(ACC[:, DS(o * W, W)], ACC[:, DS(o * W, W)], ps[s // 4][:, (s % 4) * W:(s % 4 + 1) * W],
                                                    ALU.add).then_inc(s_add, 1)

        def scale(e, k, count):
            acc = acc65 if count else acc64
            if count:
                for step in (lambda: e.tensor_scalar(cinv[k][:, :], acc65[:, :, F], 1.0, None, ALU.max),
                             lambda: e.reciprocal(cinv[k][:, :], cinv[k][:, :])):
                    nn[0] += 1
                    step().then_inc(s_n, 1)
                    e.wait_ge(s_n, nn[0])
            nn[0] += 1
            e.tensor_tensor(Hn, acc[:, :, 0:F], cinv[k][:, :].unsqueeze(2).to_broadcast([P, NB, F]), ALU.mult).then_inc(s_n, 1)

        def scale_store(k, table, count=False):
            w = nst[0]
            nst[0] += 16
            with nc.Block() as block:
                @block.vector
                def _(e):
                    scale(e, k, count)

                @block.sync
                def _(e):
                    e.wait_ge(s_n, nn[0])
                    e.dma_start(table.rearrange("(b p) f -> p b f", p=P), Hn).then_inc(s_w2, 16)
                    e.wait_ge(s_w2, w + 16)

        s_w2 = sem("s_w2")
        nst = [0]
        s_t, s_tc, s_m, s_o = sem("s_t"), sem("s_tc"), sem("s_m"), sem("s_o")
        GB = 4
        NG = NB // GB
        nlin = [0]

        def linear(name, w, finish):
            r = nlin[0]
            nlin[0] += 1
            b = r * NG
            cx = ExitStack()
            with cx:
                pt = [pst(cx, f"pt{name}{n}") for n in range(2)]
                po = [pst(cx, f"po{name}{n}") for n in range(2)]
                hT = [sbt(cx, f"hT{name}{n}", [F, GB, P], fp32) for n in range(2)]
                n = w.shape[1]
                with nc.Block() as block:
                    @block.tensor
                    def _(e):
                        for g in range(NG + 1):
                            if g < NG:
                                if g >= 2:
                                    e.wait_ge(s_tc, b + g - 1)
                                for j in range(GB):
                                    ins = e.transpose(pt[g % 2][0:F, j * P:(j + 1) * P], Hn[:, g * GB + j, :], idn[:, :])
                                ins.then_inc(s_t, 1)
                            if g >= 1:
                                q = g - 1
                                e.wait_ge(s_tc, b + q + 1)
                                if q >= 2:
                                    e.wait_ge(s_o, b + q - 1)
                                for j in range(GB):
                                    ins = e.matmul(po[q % 2][:, j * n:(j + 1) * n], lhsT=hT[q % 2][:, j, :], rhs=w[:, :], start=True, stop=True)
                                ins.then_inc(s_m, 1)

                    @block.scalar
                    def _(e):
                        for g in range(NG):
                            e.wait_ge(s_t, b + g + 1)
                            if g >= 2:
                                e.wait_ge(s_m, b + g - 1)
                            e.activation(hT[g % 2][:, :, :].rearrange("p j n -> p (j n)"), pt[g % 2][0:F, :], ACT.Copy).then_inc(s_tc, 1)

                    @block.vector
                    def _(e):
                        for g in range(NG):
                            e.wait_ge(s_m, b + g + 1)
                            finish(e, g, po[g % 2][:, 0:GB * n].rearrange("p (j n) -> p j n", n=n)).then_inc(s_o, 1)

        def bc(t, n):
            return t[:, :].unsqueeze(1).to_broadcast([P, GB, n])

        def store_block(table, v):
            w = nst[0]
            nst[0] += 16
            with nc.Block() as block:
                @block.sync
                def _(e):
                    e.dma_start(table.rearrange("(b p) f -> p b f", p=P), v).then_inc(s_w2, 16)
                    e.wait_ge(s_w2, w + 16)

        hop(tab_h, "d", True)
        scale_store("d", tab_e, True)
        hop(tab_e, "s", True)
        with nc.Block() as block:
            @block.vector
            def _(e):
                scale(e, "s", True)

        linear("a", nW["W1s"], lambda e, g, p: e.tensor_tensor(acc64[:, g * GB:(g + 1) * GB, :], p, bc(nW["b1s"], F), ALU.add))
        nn[0] += 1
        with nc.Block() as block:
            @block.vector
            def _(e):
                e.tensor_scalar(Hn, acc64, 0.0, None, ALU.max).then_inc(s_n, 1)
        store_block(tab_h, Hn)
        hop(tab_h, "d")
        scale_store("d", tab_e)
        hop(tab_e, "s")
        with nc.Block() as block:
            @block.vector
            def _(e):
                scale(e, "s", False)

        linear("b", nW["W2s"], lambda e, g, p: e.tensor_tensor(acc64[:, g * GB:(g + 1) * GB, :], p, bc(nW["b2s"], F), ALU.add))
        n0 = nn[0]
        nn[0] += 1
        with nc.Block() as block:
            na[0] += 1

            @block.scalar
            def _(e):
                ln_act(e, n0 + 6)

            @block.vector
            def _(e):
                e.tensor_tensor(X[:, :, :], X[:, :, :], acc64, ALU.add).then_inc(s_n, 1)
                e.wait_ge(s_n, n0 + 1)
                layernorm_relu(e, acc64)

        tab_n = dram("tab_n", (ROWS, F), fp32)
        store_block(tab_n, Hn)
        qx = ExitStack()
        with qx:
            Qt = sbt(qx, "Qt", [P, NB, HID], fp32)
            linear("q", nW["eW1b"], lambda e, g, p: e.tensor_copy(Qt[:, g * GB:(g + 1) * GB, :], p))
            store_block(tab_q, Qt[:, :, :])
        big = ExitStack()
        with big:
            P3 = sbt(big, "P3", [P, NB, 3, HID], bf16)
            px = ExitStack()
            with px:
                rem = [sbt(px, f"rem{n}", [P, GB, HID], fp32) for n in range(2)]
                s_sp = sem("s_sp")
                nsp = [0]

                def split(e, g, p):
                    def link(ins):
                        nsp[0] += 1
                        ins.then_inc(s_sp, 1)
                        e.wait_ge(s_sp, nsp[0])

                    bs = slice(g * GB, (g + 1) * GB)
                    link(e.tensor_copy(P3[:, bs, 0, :], p))
                    link(e.tensor_tensor(rem[0][:, :, :], p, P3[:, bs, 0, :], ALU.subtract))
                    link(e.tensor_copy(P3[:, bs, 1, :], rem[0][:, :, :]))
                    link(e.tensor_tensor(rem[1][:, :, :], rem[0][:, :, :], P3[:, bs, 1, :], ALU.subtract))
                    return e.tensor_copy(P3[:, bs, 2, :], rem[1][:, :, :])

                linear("p", nW["eW1a"], split)

            l_rec = [sem(f"l_rec{h}") for h in range(2)]
            l_oh, l_w, l_t, l_tc, l_p, l_y, l_2, l_zb, l_z, l_a, l_add = (
                sem(f"l_{n}") for n in ("oh", "w", "t", "tc", "p", "y", "2", "zb", "z", "a", "add"))
            b_g = nhop[0] * TURNS * 16
            rv = recs["s"].rearrange("(s t) c -> s t c", s=P)
            cx = ExitStack()
            with cx:
                G = sbt(cx, "GL", [P, BODY, HID], fp32)
                rb = [sbt(cx, f"rbL{h}", [P, HT, 4], i32) for h in range(2)]
                tb = [sbt(cx, f"tbL{h}", [1, HT], i32) for h in range(2)]
                O = [sbt(cx, f"OL{h}", [P, HT, P], fp32) for h in range(2)]
                ST = [sbt(cx, f"ST{n}", [P, 512], bf16) for n in range(2)]
                Y = sbt(cx, "Y", [P, 512], fp32)
                Zb = sbt(cx, "Zb", [P, 512], fp32)
                Z = sbt(cx, "Z", [P, 512], fp32)
                pT = [pst(cx, f"pT{n}") for n in range(2)]
                pP = [pst(cx, f"pP{n}") for n in range(2)]
                p2 = [pst(cx, f"p2{n}") for n in range(2)]
                pA = [pst(cx, f"pA{n}") for n in range(2)]
                Pf = P3[:, :, :, :].rearrange("p b c h -> p (b c h)")
                NGL = BODY // 4

                def done(e, s, i, g):
                    e.wait_ge(s, i * NGL + (g + 3))

                with nc.Block() as block:
                    @block.sync
                    def _(e):
                        with e.Fori(0, TURNS) as i:
                            for h in range(2):
                                e.wait_ge(l_add, i * BODY + (1 + h * HT))
                                e.dma_start(rb[h][:, :, :], rv[:, DS(i * BODY + h * HT, HT), :]).then_inc(l_rec[h], 16)
                                e.dma_start(tb[h][:, :], tofs["s"][DS(i * 2 + h, 1), :]).then_inc(l_rec[h], 16)

                    @block.gpsimd
                    def _(e):
                        with e.Fori(0, TURNS) as i:
                            for h in range(2):
                                wait_here(e, l_rec[h], i * 32 + 32)
                                for t in range(HT):
                                    s = h * HT + t
                                    e.indirect_dma_start(G[:, s, :], None, tab_q,
                                                         bass.IndirectOffsetOnAxis(ap=rb[h][:, t, 0:1], axis=0)).then_inc(s_g[s], 16)

                    @block.tensor
                    def _(e):
                        for s in (l_t, l_p, l_2, l_a):
                            e.sem_inc(s, 2)
                        regs = [e.alloc_register(f"lp_{n}") for n in range(HT)]
                        with e.Fori(0, TURNS) as i:
                            def stage_t(g):
                                if g % 4 == 0:
                                    e.wait_ge(l_oh, i * 2 + (g // 4 + 1))
                                done(e, l_tc, i, g - 2)
                                for j in range(4):
                                    ins = e.transpose(pT[g % 2][:, j * P:(j + 1) * P], O[g // 4][:, (g % 4) * 4 + j, :], idn[:, :])
                                ins.then_inc(l_t, 1)

                            def stage_p(g):
                                if g % 4 == 0:
                                    e.load(regs, tb[g // 4][0:1, :])
                                done(e, l_tc, i, g)
                                done(e, l_w, i, g)
                                done(e, l_y, i, g - 2)
                                for j in range(4):
                                    s = g * 4 + j
                                    o = e.snap(regs[(g % 4) * 4 + j], min_val=0, max_val=NB - 1)
                                    for c in range(3):
                                        e.matmul(pP[g % 2][:, j * P:(j + 1) * P], lhsT=Pf[:, DS(o * (3 * HID) + c * HID, HID)],
                                                 rhs=ST[g % 2][:, j * P:(j + 1) * P], start=c == 0, stop=False)
                                    ins = e.matmul(pP[g % 2][:, j * P:(j + 1) * P], lhsT=G[:, s, :], rhs=idn[:, :], start=False, stop=True)
                                ins.then_inc(l_p, 1)

                            def stage_2(g):
                                done(e, l_y, i, g)
                                done(e, l_zb, i, g - 2)
                                for j in range(4):
                                    ins = e.matmul(p2[g % 2][:, j * P:(j + 1) * P], lhsT=Y[:, j * P:(j + 1) * P], rhs=nW["eW2s"][:, :],
                                                   start=True, stop=True)
                                ins.then_inc(l_2, 1)

                            def stage_a(g):
                                done(e, l_z, i, g)
                                e.wait_ge(l_add, i * BODY + (17 + g * 4 - 4))
                                for j in range(4):
                                    ins = e.matmul(pA[g % 2][:, j * P:(j + 1) * P], lhsT=O[g // 4][:, (g % 4) * 4 + j, :],
                                                   rhs=Z[:, j * P:(j + 1) * P], start=True, stop=True)
                                ins.then_inc(l_a, 1)

                            for g in range(NGL + 3):
                                if g < NGL:
                                    stage_t(g)
                                if 1 <= g <= NGL:
                                    stage_p(g - 1)
                                if 2 <= g <= NGL + 1:
                                    stage_2(g - 2)
                                if 3 <= g:
                                    stage_a(g - 3)

                    @block.scalar
                    def _(e):
                        for s in (l_tc, l_y, l_z):
                            e.sem_inc(s, 2)
                        with e.Fori(0, TURNS) as i:
                            def copy_t(g):
                                done(e, l_t, i, g)
                                done(e, l_p, i, g - 2)
                                e.activation(ST[g % 2][:, :], pT[g % 2][:, :], ACT.Copy).then_inc(l_tc, 1)

                            for g in range(NGL + 2):
                                if g < NGL:
                                    copy_t(g)
                                if 1 <= g <= NGL:
                                    q = g - 1
                                    done(e, l_p, i, q)
                                    done(e, l_2, i, q - 1)
                                    e.activation(Y[:, :], pP[q % 2][:, :], ACT.Silu, bias=nW["eb1s"][:, 0:1]).then_inc(l_y, 1)
                                if 2 <= g:
                                    q = g - 2
                                    done(e, l_zb, i, q)
                                    done(e, l_a, i, q - 1)
                                    e.activation(Z[:, :], Zb[:, :], ACT.Silu).then_inc(l_z, 1)

                    @block.vector
                    def _(e):
                        e.memset(ACC[:, 0:NB * HID], 0.0).then_inc(l_add, 17)
                        e.sem_inc(l_zb, 2)
                        e.sem_inc(l_w, 2)
                        regs = [e.alloc_register(f"la_{n}") for n in range(HT)]
                        with e.Fori(0, TURNS) as i:
                            def onehot(h):
                                e.wait_ge(l_rec[h], i * 32 + 32)
                                e.tensor_tensor(O[h][:, :, :], rb[h][:, :, 1:2].bitcast(fp32).to_broadcast([P, HT, P]),
                                                iota[:, :].unsqueeze(1).to_broadcast([P, HT, P]), ALU.is_equal).then_inc(l_oh, 1)

                            def weight(g):
                                for j in range(4):
                                    s = g * 4 + j
                                    e.wait_ge(s_g[s], i * 16 + (b_g + 16))
                                    ins = e.scalar_tensor_tensor(G[:, s, :], nW["w1b"][:, :], rb[s // HT][:, s % HT, 2:3].bitcast(fp32),
                                                                 G[:, s, :], ALU.mult, ALU.add)
                                ins.then_inc(l_w, 1)

                            def bias2(g):
                                done(e, l_2, i, g)
                                done(e, l_z, i, g - 1)
                                e.tensor_tensor(Zb[:, :].rearrange("p (j n) -> p j n", n=HID), p2[g % 2][:, :].rearrange("p (j n) -> p j n", n=HID),
                                                nW["eb2s"][:, :].unsqueeze(1).to_broadcast([P, 4, HID]), ALU.add).then_inc(l_zb, 1)

                            def add(g):
                                if g % 4 == 0:
                                    e.load(regs, tb[g // 4][0:1, :])
                                done(e, l_a, i, g)
                                for j in range(4):
                                    s = g * 4 + j
                                    o = e.snap(regs[s % HT], min_val=0, max_val=NB - 1)
                                    e.wait_ge(l_add, i * BODY + (17 + s))
                                    e.tensor_tensor(ACC[:, DS(o * HID, HID)], ACC[:, DS(o * HID, HID)], pA[g % 2][:, j * P:(j + 1) * P],
                                                    ALU.add).then_inc(l_add, 1)

                            for g in range(NGL + 3):
                                if g == 0:
                                    onehot(0)
                                if g < NGL:
                                    weight(g)
                                if g == 2:
                                    onehot(1)
                                if 2 <= g <= NGL + 1:
                                    bias2(g - 2)
                                if 3 <= g:
                                    add(g - 3)

        fx = ExitStack()
        with fx:
            H1 = sbt(fx, "H1", [P, NB, F], fp32)
            OUT = sbt(fx, "OUT", [P, NB, F], fp32)
            hT = [sbt(fx, f"fhT{n}", [F, 512], fp32) for n in range(2)]
            aT = [sbt(fx, f"faT{n}", [P, 512], fp32) for n in range(2)]
            u = [sbt(fx, f"fu{n}", [P, 512], fp32) for n in range(2)]
            ph = pst(fx, "ph")
            pa = pst(fx, "pa")
            pu = [pst(fx, f"pu{n}") for n in range(2)]
            po = [pst(fx, f"pof{n}") for n in range(2)]
            f_l, f_t, f_hc, f_ac, f_u, f_s, f_o, f_v, f_b = (sem(f"f_{n}") for n in ("l", "t", "hc", "ac", "u", "s", "o", "v", "b"))
            with nc.Block() as block:
                @block.sync
                def _(e):
                    e.dma_start(H1[:, :, :], tab_n.rearrange("(b p) f -> p b f", p=P)).then_inc(f_l, 16)
                    e.wait_ge(f_v, NG)
                    e.dma_start(out[0:97 * P, :].rearrange("(b p) f -> p b f", p=P), OUT[:, 0:97, :]).then_inc(f_l, 16)
                    e.dma_start(out[97 * P:N_NODES, :], OUT[0:N_NODES - 97 * P, 97, :]).then_inc(f_l, 16)
                    e.wait_ge(f_l, 48)

                @block.tensor
                def _(e):
                    e.wait_ge(f_l, 16)
                    for g in range(NG + 2):
                        if g < NG:
                            e.wait_ge(f_hc, g)
                            e.wait_ge(f_ac, g)
                            for j in range(GB):
                                e.transpose(ph[0:F, j * P:(j + 1) * P], H1[:, g * GB + j, :], idn[:, :])
                                ins = e.transpose(pa[:, j * P:(j + 1) * P], ACC[:, (g * GB + j) * HID:(g * GB + j + 1) * HID], idn[:, :])
                            ins.then_inc(f_t, 1)
                        if 1 <= g <= NG:
                            q = g - 1
                            e.wait_ge(f_hc, q + 1)
                            e.wait_ge(f_ac, q + 1)
                            if q >= 2:
                                e.wait_ge(f_s, q - 1)
                            e.matmul(pu[q % 2][:, :], lhsT=nW["nW1a"][:, :], rhs=hT[q % 2][:, :], start=True, stop=False)
                            e.matmul(pu[q % 2][:, :], lhsT=nW["nW1b"][:, :], rhs=aT[q % 2][:, :], start=False, stop=True).then_inc(f_u, 1)
                        if 2 <= g:
                            q = g - 2
                            e.wait_ge(f_s, q + 1)
                            if q >= 2:
                                e.wait_ge(f_v, q - 1)
                            for j in range(GB):
                                ins = e.matmul(po[q % 2][:, j * F:(j + 1) * F], lhsT=u[q % 2][:, j * P:(j + 1) * P], rhs=nW["nW2s"][:, :],
                                               start=True, stop=True)
                            ins.then_inc(f_o, 1)

                @block.scalar
                def _(e):
                    for g in range(NG + 1):
                        if g < NG:
                            e.wait_ge(f_t, g + 1)
                            if g >= 2:
                                e.wait_ge(f_u, g - 1)
                            e.activation(hT[g % 2][:, :], ph[0:F, :], ACT.Copy).then_inc(f_hc, 1)
                        if g >= 1:
                            q = g - 1
                            e.wait_ge(f_u, q + 1)
                            if q >= 2:
                                e.wait_ge(f_o, q - 1)
                            e.activation(u[q % 2][:, :], pu[q % 2][:, :], ACT.Silu, bias=nW["nb1s"][:, 0:1]).then_inc(f_s, 1)

                @block.vector
                def _(e):
                    for g in range(NG + 2):
                        if g < NG:
                            e.wait_ge(f_t, g + 1)
                            if g >= 2:
                                e.wait_ge(f_u, g - 1)
                            e.tensor_copy(aT[g % 2][:, :], pa[:, :]).then_inc(f_ac, 1)
                        if g >= 2:
                            q = g - 2
                            v = OUT[:, q * GB:(q + 1) * GB, :]
                            e.wait_ge(f_o, q + 1)
                            e.tensor_tensor(v, po[q % 2][:, 0:GB * F].rearrange("p (j n) -> p j n", n=F), bc(nW["nb2s"], F),
                                            ALU.add).then_inc(f_b, 1)
                            e.wait_ge(f_b, q + 1)
                            e.tensor_tensor(v, v, X[:, q * GB:(q + 1) * GB, :], ALU.add).then_inc(f_v, 1)


_INS = ['x', 'src', 'dst', 'edge_weight1', 'L0_gnn_W1', 'L0_gnn_b1', 'L0_gnn_W2', 'L0_gnn_b2', 'L1_gnn_eW1', 'L1_gnn_eb1',
        'L1_gnn_eW2', 'L1_gnn_eb2', 'L1_gnn_nW1', 'L1_gnn_nb1', 'L1_gnn_nW2', 'L1_gnn_nb2']


def kernel(**inputs):
    import numpy as np
    import concourse.bacc as bacc
    from concourse import mybir as mb
    from concourse.bass_utils import run_bass_kernel_spmd

    nc = bacc.Bacc("TRN2", target_bir_lowering=False, num_devices=1)
    arrays, args = {}, []
    for name in _INS:
        a = np.ascontiguousarray(inputs[name])
        if name == "edge_weight1":
            a = a.reshape(N_EDGES)
        arrays[f"in_{name}"] = a
        args.append(nc.dram_tensor(f"in_{name}", a.shape, mb.dt.from_np(a.dtype), kind="ExternalInput").ap())
    args.append(nc.dram_tensor("out_0", (N_NODES, F), mb.dt.float32, kind="ExternalOutput").ap())
    gnn_kernel(nc, *args)
    r = run_bass_kernel_spmd(nc, [arrays], core_ids=[0])
    return r.results[0]["out_0"]
```

```python
import concourse.bass as bass
from concourse import mybir
from contextlib import ExitStack

N_NODES = 12500
N_EDGES = 412500
P = 128
NB = 100
ROWS = NB * P
TI = 3224
LAST = N_EDGES - 127 * TI
PAD = 98 * P
GRP = 4
SB_GROUPS = 26
SB = GRP * SB_GROUPS
S_TURNS = TI // SB
EP = TI * P
ND = 99
ACT_KEYS = 78
HALF_G = SB_GROUPS // 2
HALF_T = SB // 2
NT = 3328
BODY = 32
HT = 16
TURNS = NT // BODY
NC = NT // P
F = 64
HID = 128


def gnn_kernel(nc, x, src, dst, ew, W1, b1, W2, b2, eW1, eb1, eW2, eb2, nW1, nb1, nW2, nb2, out):
    fp32 = mybir.dt.float32
    bf16 = mybir.dt.bfloat16
    i32 = mybir.dt.int32
    ALU = mybir.AluOpType
    ACT = mybir.ActivationFunctionType
    AX = mybir.AxisListType.X
    DS = bass.ds

    root = ExitStack()
    with root:
        def sem(name):
            return root.enter_context(nc.semaphore(name))

        s_mark = sem("s_mark")

        def wait_here(e, s, v):
            e.wait_ge(s, v)
            e.sem_inc(s_mark, 1)

        def sbt(ctx, name, shape, dt):
            return ctx.enter_context(nc.sbuf_tensor(name, shape, dt))

        def pst(ctx, name, dt=fp32):
            return ctx.enter_context(nc.psum_tensor(name, [P, 512 if dt == fp32 else 1024], dt))

        def dram(name, shape, dt):
            return nc.dram_tensor(name, shape, dt).ap()

        recs = {"d": dram("rec_d", (P * NT, 4), i32), "s": dram("rec_s", (P * NT, 4), i32)}
        tofs = {"d": dram("tof_d", (TURNS * 2, HT), i32), "s": dram("tof_s", (TURNS * 2, HT), i32)}
        recT = dram("rec_t", (NT, 2 * P), i32)
        SD = dram("pairs", (1, 2 * EP + 2 * P), i32)
        e0d = dram("e0d", (1, NT), i32)
        tab_h = dram("tab_h", (ROWS, F), fp32)
        tab_e = dram("tab_e", (ROWS, F), fp32)
        tab_q = dram("tab_q", (ROWS, HID), fp32)

        X = sbt(root, "X", [P, NB, F], fp32)
        ACC = sbt(root, "ACC", [P, NB * (2 * F + 1)], fp32)
        acc64 = ACC[:, 0:NB * F].rearrange("p (b f) -> p b f", f=F)
        acc65 = ACC[:, 0:NB * (F + 1)].rearrange("p (b f) -> p b f", f=F + 1)
        Hn = ACC[:, NB * (F + 1):NB * (2 * F + 1)].rearrange("p (b f) -> p b f", f=F)
        idn = sbt(root, "idn", [P, P], fp32)
        iota = sbt(root, "iota", [P, P], fp32)
        idb = sbt(root, "idb", [P, P], bf16)
        iotb = sbt(root, "iotb", [P, P], bf16)
        cinv = {"d": sbt(root, "cinv_d", [P, NB], fp32), "s": sbt(root, "cinv_s", [P, NB], fp32)}
        eps = sbt(root, "eps", [P, 1], fp32)

        sm = {n: sbt(root, f"ln_{n}", [P, NB], fp32) for n in ("m", "v")}
        s_n = sem("s_n")
        s_na = sem("s_na")
        s_w = sem("s_w")
        s_h0 = sem("s_h0")
        nn = [0]
        na = [0]

        def layernorm_relu(e, sq):
            def link(ins):
                nn[0] += 1
                ins.then_inc(s_n, 1)
                e.wait_ge(s_n, nn[0])

            link(e.tensor_reduce(sm["m"][:, :], X[:, :, :], AX, ALU.add))
            link(e.tensor_scalar(sm["m"][:, :], sm["m"][:, :], 1.0 / F, None, ALU.mult))
            link(e.tensor_tensor(Hn, X[:, :, :], sm["m"][:, :].unsqueeze(2).to_broadcast([P, NB, F]), ALU.subtract))
            link(e.tensor_tensor(sq, Hn, Hn, ALU.mult))
            link(e.tensor_reduce(sm["v"][:, :], sq, AX, ALU.add))
            e.wait_ge(s_na, na[0])
            link(e.reciprocal(sm["v"][:, :], sm["m"][:, :]))
            link(e.tensor_tensor(Hn, Hn, sm["v"][:, :].unsqueeze(2).to_broadcast([P, NB, F]), ALU.mult))
            link(e.tensor_scalar(Hn, Hn, 0.0, None, ALU.max))

        def ln_act(e, target):
            e.wait_ge(s_n, target)
            e.activation(sm["m"][:, :], sm["v"][:, :], ACT.Sqrt, bias=eps[:, 0:1], scale=1.0 / F).then_inc(s_na, 1)

        s_ld, s_fill, s_c, s_pc = sem("s_ld"), sem("s_fill"), sem("s_c"), sem("s_pc")
        s_k, s_km, s_ka = sem("s_k"), sem("s_km"), sem("s_ka")
        st = ExitStack()
        with st:
            E = {"s": sbt(st, "E_s", [P, TI + 1], i32), "d": sbt(st, "E_d", [P, TI + 1], i32)}
            Wt = sbt(st, "Wt", [P, TI], fp32)
            HI = {k: sbt(st, f"HI_{k}", [P, TI], bf16) for k in "sd"}
            LO = {k: sbt(st, f"LO_{k}", [P, TI], bf16) for k in "sd"}
            pair = ACC[:, 0:2 * TI].bitcast(i32).rearrange("p (t c) -> p t c", c=2)
            itmp = ACC[:, 2 * TI:3 * TI].bitcast(i32)
            junkb = ACC[:, 3 * TI:3 * TI + TI // 2].bitcast(bf16)
            junka = ACC[:, 0:TI // 2].bitcast(bf16)
            tail = sbt(st, "tail", [1, 2 * P], i32)
            U = sbt(st, "U", [P, P], bf16)
            ones = sbt(st, "ones", [P, P], bf16)
            onef = sbt(st, "onef", [P, P], fp32)
            fill = sbt(st, "fill", [P, 416, 4], i32)
            oh = [sbt(st, f"oh{n}", [P, GRP, P], bf16) for n in range(2)]
            tmp = sbt(st, "tmp", [P, GRP, P], fp32)
            junk = sbt(st, "junk", [P, P], fp32)
            pos = sbt(st, "pos", [P, SB], fp32)
            posi = sbt(st, "posi", [P, HALF_T], i32)
            sloti = sbt(st, "sloti", [P, HALF_T], i32)
            idx = [sbt(st, f"idx{n}", [P, HALF_T], i32) for n in range(2)]
            rec = [sbt(st, f"rec{n}", [P, HALF_T, 4], i32) for n in range(2)]
            scr = [sbt(st, f"scr{n}", [1, 16], i32) for n in range(2)]
            run = {k: sbt(st, f"run_{k}", [P, P], fp32) for k in "sd"}
            cum = {k: sbt(st, f"cum_{k}", [P, NB], fp32) for k in "sd"}
            Tt = sbt(st, "Tt", [P, NC], fp32)
            bT = {k: sbt(st, f"bT_{k}", [P, NC], fp32) for k in "sd"}
            e0 = sbt(st, "e0", [P, NC], fp32)
            c99 = {n: sbt(st, f"c99_{n}", [P, ND], fp32) for n in ("cnt", "nt", "tb", "st", "base", "delta", "z", "bias")}
            c99i = sbt(st, "c99i", [P, ND], i32)
            bad = sbt(st, "bad", [P, 1], fp32)
            badi = sbt(st, "badi", [P, 1], i32)
            rows = {n: sbt(st, f"rows_{n}", [NC, P], i32) for n in ("s", "d", "e")}
            e0s = [sbt(st, f"e0s{n}", [1, NT], i32) for n in range(2)]

            with nc.Block() as block:
                @block.sync
                def _(e):
                    e.wait_ge(s_c, 3)
                    for t, a in ((E["s"], src), (E["d"], dst), (Wt, ew)):
                        e.dma_start(t[0:127, 0:TI], a[0:127 * TI].rearrange("(p t) -> p t", t=TI)).then_inc(s_ld, 16)
                        e.dma_start(t[127:128, 0:LAST], a[127 * TI:N_EDGES].rearrange("(a t) -> a t", a=1)).then_inc(s_ld, 16)
                    with nc.allow_non_contiguous_dma(reason="127 elements"):
                        e.dma_start(E["d"][0:127, TI:TI + 1], dst[TI:].rearrange("(a n) -> a n", a=1)[0:1, 0:126 * TI + 1:TI].rearrange("a n -> n a")).then_inc(s_ld, 16)
                    e.wait_ge(s_c, 4)
                    e.dma_start(X[:, 0:97, :], x[0:97 * P, :].rearrange("(b p) f -> p b f", p=P)).then_inc(s_ld, 16)
                    e.dma_start(X[0:N_NODES - 97 * P, 97, :], x[97 * P:N_NODES, :]).then_inc(s_ld, 16)
                    e.wait_ge(s_fill, 3)
                    v = recs["s"].rearrange("(p t) c -> p t c", p=P)
                    for j in range(8):
                        e.dma_start(v[:, j * 416:(j + 1) * 416, :], fill[:, :, :]).then_inc(s_pc, 16)
                    e.wait_ge(s_c, 6)
                    e.dma_start(SD[0:1, 0:2 * EP].rearrange("a (p t) -> (a p) t", p=P), ACC[:, 0:2 * TI].bitcast(i32)).then_inc(s_pc, 16)
                    e.dma_start(SD[0:1, 2 * EP:2 * EP + 2 * P], tail[:, :]).then_inc(s_pc, 16)
                    e.wait_ge(s_ld, 144)
                    e.wait_ge(s_pc, 160)

                @block.vector
                def _(e):
                    e.memset(E["s"][:, :], PAD).then_inc(s_c, 1)
                    e.memset(E["d"][:, :], PAD).then_inc(s_c, 1)
                    e.memset(Wt[:, :], 0.0).then_inc(s_c, 1)
                    e.memset(X[:, :, :], 0.0).then_inc(s_c, 1)
                    e.memset(eps[:, :], 1e-5)
                    e.memset(c99["z"][:, :], 0.0)
                    e.memset(tail[:, :], PAD + P).then_inc(s_k, 1)
                    e.memset(rec[0][:, :, 3], 0)
                    e.memset(rec[1][:, :, 3], 0)
                    e.wait_ge(s_ld, 144)
                    e.tensor_copy(pair[:, :, 0], E["s"][:, 0:TI]).then_inc(s_c, 1)
                    e.tensor_copy(pair[:, :, 1], E["d"][:, 0:TI]).then_inc(s_c, 1)
                    n = 6
                    for k in "sd":
                        e.tensor_scalar(itmp, E[k][:, 0:TI], 7, None, ALU.arith_shift_right).then_inc(s_c, 1)
                        e.wait_ge(s_c, n + 1)
                        e.tensor_copy(HI[k][:, :], itmp).then_inc(s_c, 1)
                        e.wait_ge(s_c, n + 2)
                        e.tensor_scalar(itmp, E[k][:, 0:TI], 127, None, ALU.bitwise_and).then_inc(s_c, 1)
                        e.wait_ge(s_c, n + 3)
                        e.tensor_copy(LO[k][:, :], itmp).then_inc(s_c, 1)
                        e.wait_ge(s_c, n + 4)
                        n += 4

                @block.gpsimd
                def _(e):
                    e.iota(iota[:, :], pattern=[[1, P]], base=0, channel_multiplier=0,
                           allow_small_or_imprecise_dtypes=True).then_inc(s_fill, 1)
                    e.iota(Tt[:, :], pattern=[[P, NC]], base=0, channel_multiplier=1, allow_small_or_imprecise_dtypes=True)
                    e.memset(fill[:, :, 1:4], 0).then_inc(s_fill, 1)
                    e.wait_ge(s_fill, 2)
                    e.memset(fill[:, :, 0:1], PAD)
                    e.memset(fill[:, :, 1:2].bitcast(fp32), -1.0).then_inc(s_fill, 1)
                    e.wait_ge(s_fill, 3)
                    e.tensor_copy(iotb[:, :], iota[:, :]).then_inc(s_fill, 1)
                    e.memset(ones[:, :], 1.0).then_inc(s_fill, 1)
                    e.memset(onef[:, :], 1.0)
                    e.memset(idn[:, :], 0.0).then_inc(s_fill, 1)
                    e.memset(U[:, :], 1.0).then_inc(s_fill, 1)
                    e.wait_ge(s_fill, 7)
                    e.affine_select(out=U[:, :], in_=U[:, :], compare_op=ALU.is_gt, fill=0.0, base=0,
                                    pattern=[[1, P]], channel_multiplier=-1)
                    e.affine_select(out=idn[:, :], in_=idn[:, :], compare_op=ALU.not_equal, fill=1.0, base=0,
                                    pattern=[[-1, P]], channel_multiplier=1).then_inc(s_fill, 1)
                    e.wait_ge(s_fill, 8)
                    e.tensor_copy(idb[:, :], idn[:, :])

            kx = ExitStack()
            with kx:
                ge, gd = (ACC[:, n * NC * ND:(n + 1) * NC * ND].rearrange("p (c b) -> p c b", b=ND) for n in range(2))
                pk = pst(kx, "pk")
                pr = pst(kx, "pr")
                kn = [1]
                with nc.Block() as block:
                    @block.vector
                    def _(e):
                        def link(ins):
                            kn[0] += 1
                            ins.then_inc(s_k, 1)
                            e.wait_ge(s_k, kn[0])

                        def clear(k):
                            e.memset(cum[k][:, 0:1], float(TI))
                            link(e.memset(cum[k][:, ND:NB], 0.0))

                        for k in "sd":
                            clear(k)
                        e.tensor_scalar(c99["bias"][:, :], iota[:, 0:ND], -1.0, 0.5, ALU.mult, ALU.add).then_inc(s_ka, 1)
                        link(e.tensor_tensor(itmp, E["d"][:, 1:TI + 1], E["d"][:, 0:TI], ALU.is_lt))
                        link(e.tensor_reduce(bad[:, :], itmp, AX, ALU.max))
                        for k in "sd":
                            for b in range(1 if k == "s" else ACT_KEYS, ND):
                                link(e.tensor_scalar(junkb, HI[k][:, :], float(b), 0.0, ALU.is_ge, ALU.add, accum_out=cum[k][:, b:b + 1]))
                        e.wait_ge(s_ka, ACT_KEYS)
                        link(e.tensor_scalar(cum["d"][:, 1:ACT_KEYS], cum["d"][:, 1:ACT_KEYS], 0.5, TI * 0.5, ALU.mult, ALU.add))
                        e.sem_inc(s_km, 1)
                        e.wait_ge(s_km, 2)
                        for k in "ds":
                            tot = pk[:, 0:NB] if k == "d" else pk[:, 128:128 + NB]
                            c = c99
                            link(e.tensor_copy(cum[k][:, :], tot))
                            link(e.tensor_tensor(c["cnt"][:, :], cum[k][:, 0:ND], cum[k][:, 1:NB], ALU.subtract))
                            link(e.tensor_scalar(c["cnt"][:, :], c["cnt"][:, :], 127.0, None, ALU.add))
                            link(e.tensor_copy(c99i[:, :], c["cnt"][:, :]))
                            link(e.tensor_scalar(c99i[:, :], c99i[:, :], 7, None, ALU.arith_shift_right))
                            link(e.tensor_copy(c["nt"][:, :], c99i[:, :]))
                            link(e.tensor_tensor_scan(c["tb"][:, :], c["nt"][:, :], c["z"][:, :], 0.0, ALU.add, ALU.add))
                            link(e.tensor_tensor(c["tb"][:, :], c["tb"][:, :], c["nt"][:, :], ALU.subtract))
                            link(e.memset(run[k][:, :], 0.0))
                            link(e.tensor_scalar(run[k][:, 0:ND], c["tb"][:, :], 128.0, None, ALU.mult))
                            link(e.tensor_tensor(ge[:, :, :], Tt[:, :].unsqueeze(2).to_broadcast([P, NC, ND]),
                                                 c["tb"][:, :].unsqueeze(1).to_broadcast([P, NC, ND]), ALU.is_ge))
                            link(e.tensor_reduce(bT[k][:, :], ge[:, :, :], AX, ALU.add))
                            link(e.tensor_scalar(bT[k][:, :], bT[k][:, :], -1.0, None, ALU.add))
                            if k == "d":
                                link(e.scalar_tensor_tensor(c["st"][:, :], cum[k][:, 0:ND], -1.0,
                                                            cum[k][:, 0:1].to_broadcast([P, ND]), ALU.mult, ALU.add))
                                link(e.tensor_tensor(c["base"][:, :], c["st"][:, :], run[k][:, 0:ND], ALU.subtract))
                                link(e.tensor_copy(c["delta"][:, :], c["base"][:, :]))
                                link(e.tensor_tensor(c["delta"][:, 1:ND], c["base"][:, 1:ND], c["base"][:, 0:ND - 1], ALU.subtract))
                                link(e.tensor_tensor(gd[:, :, :], ge[:, :, :], c["delta"][:, :].unsqueeze(1).to_broadcast([P, NC, ND]),
                                                     ALU.mult))
                                link(e.tensor_reduce(e0[:, :], gd[:, :, :], AX, ALU.add))
                                link(e.scalar_tensor_tensor(e0[:, :], Tt[:, :], 128.0, e0[:, :], ALU.mult, ALU.add))
                                link(e.tensor_scalar(e0[:, :], e0[:, :], float(EP), 0.0, ALU.min, ALU.max))
                                link(e.tensor_scalar(badi[:, 0:1], pk[:, 256:257], 0.5, None, ALU.is_ge))
                        e.sem_inc(s_km, 1)
                        e.wait_ge(s_km, 4)
                        for n, k in enumerate("sde"):
                            link(e.tensor_copy(rows[k][:, :], pr[0:NC, n * P:(n + 1) * P]))

                    @block.scalar
                    def _(e):
                        for b in range(1, ACT_KEYS):
                            e.wait_ge(s_ka, b)
                            e.activation(junka, HI["d"][:, :], ACT.Sign, bias=c99["bias"][:, b:b + 1],
                                         accum_out=cum["d"][:, b:b + 1]).then_inc(s_ka, 1)

                    @block.tensor
                    def _(e):
                        e.wait_ge(s_km, 1)
                        e.matmul(pk[:, 0:NB], lhsT=onef[:, :], rhs=cum["d"][:, :], start=True, stop=True)
                        e.matmul(pk[:, 256:257], lhsT=onef[:, :], rhs=bad[:, :], start=True, stop=True)
                        e.matmul(pk[:, 128:128 + NB], lhsT=onef[:, :], rhs=cum["s"][:, :], start=True, stop=True).then_inc(s_km, 1)
                        e.wait_ge(s_km, 3)
                        e.transpose(pr[0:NC, 0:P], bT["s"][:, :], idn[:, :])
                        e.transpose(pr[0:NC, P:2 * P], bT["d"][:, :], idn[:, :])
                        e.transpose(pr[0:NC, 2 * P:3 * P], e0[:, :], idn[:, :]).then_inc(s_km, 1)
                z0 = sem("z0")
                with nc.Block() as block:
                    @block.sync
                    def _(e):
                        for k in "sd":
                            e.dma_start(tofs[k].rearrange("(c a) t -> c (a t)", c=NC), rows[k][:, :]).then_inc(z0, 16)
                        e.dma_start(e0d.rearrange("a (c t) -> (a c) t", c=NC), rows["e"][:, :]).then_inc(z0, 16)
                        e.wait_ge(z0, 48)
                        for n in range(2):
                            e.dma_start(e0s[n][:, :], e0d).then_inc(z0, 16)
                        e.wait_ge(z0, 80)

            def onehots(e, to, frm, i, g):
                v = frm[:, DS(i * SB + g * GRP, GRP)]
                return e.tensor_tensor(to[:, :, :], v.unsqueeze(2).to_broadcast([P, GRP, P]),
                                       iotb[:, :].unsqueeze(1).to_broadcast([P, GRP, P]), ALU.is_equal)

            def sort(key, other, guard=None, beside=None):
                def guarded(body):
                    def program(e):
                        if guard is None:
                            body(e)
                        else:
                            with e.If(guard(e)):
                                body(e)
                    return program

                q_oh, q_r, q_v, q_i = sem(f"q_oh{key}"), sem(f"q_r{key}"), sem(f"q_v{key}"), sem(f"q_i{key}")
                q_s = [sem(f"q_s{key}{n}") for n in range(2)]
                NV = SB_GROUPS * 6 + 2 * 7
                px = ExitStack()
                with px:
                    R = [pst(px, f"R{key}{n}") for n in range(2)]
                    T = [pst(px, f"T{key}{n}") for n in range(2)]
                    rn = run[key]
                    with nc.Block() as block:
                        @block.vector
                        @guarded
                        def _(e):
                            e.sem_inc(q_v, 1)
                            with e.Fori(0, S_TURNS) as i:
                                n = 0

                                def did(ins):
                                    nonlocal n
                                    ins.then_inc(q_v, 1)
                                    n += 1
                                    return n

                                def need(v):
                                    e.wait_ge(q_v, i * NV + (v + 1))

                                for g in range(SB_GROUPS):
                                    need(n)
                                    if g == 0:
                                        e.wait_ge(q_r, i * SB_GROUPS + 1)
                                        onehots(e, oh[0], HI[key], i, 0).then_inc(q_oh, 1)
                                    if g + 1 < SB_GROUPS:
                                        e.wait_ge(q_r, i * SB_GROUPS + (g + 1))
                                        onehots(e, oh[(g + 1) % 2], HI[key], i, g + 1).then_inc(q_oh, 1)
                                    e.wait_ge(q_r, i * SB_GROUPS + (g + 2))
                                    a = did(e.tensor_tensor(tmp[:, :, :], R[g % 2][:, :].rearrange("p (g d) -> p g d", g=GRP),
                                                            rn[:, :].unsqueeze(1).to_broadcast([P, GRP, P]), ALU.add))
                                    need(a)
                                    for k in range(GRP):
                                        if k:
                                            need(n)
                                        did(e.tensor_tensor_reduce(out=junk[:, :], in0=tmp[:, k, :], in1=oh[g % 2][:, k, :],
                                                                   scale=1.0, scalar=0.0, op0=ALU.mult, op1=ALU.add,
                                                                   accum_out=pos[:, g * GRP + k:g * GRP + k + 1]))
                                    did(e.tensor_tensor(rn[:, :], rn[:, :], T[g % 2][:, 0:P], ALU.add))
                                    if g % HALF_G == HALF_G - 1:
                                        h = g // HALF_G
                                        t0 = i * SB + h * HALF_T
                                        need(n)
                                        e.wait_ge(q_s[h], i * (HALF_T * 16) + 16)
                                        a = did(e.tensor_copy(posi[:, :], pos[:, h * HALF_T:(h + 1) * HALF_T]))
                                        need(a)
                                        did(e.tensor_scalar(sloti[:, :], posi[:, :], 127, None, ALU.bitwise_and))
                                        a = did(e.tensor_scalar(posi[:, :], posi[:, :], 7, None, ALU.arith_shift_right))
                                        need(a)
                                        did(e.scalar_tensor_tensor(idx[h][:, :], sloti[:, :], float(NT), posi[:, :], ALU.mult, ALU.add))
                                        did(e.tensor_copy(rec[h][:, :, 0], E[other][:, DS(t0, HALF_T)]))
                                        did(e.tensor_copy(rec[h][:, :, 1].bitcast(fp32), LO[key][:, DS(t0, HALF_T)]))
                                        a = did(e.tensor_copy(rec[h][:, :, 2].bitcast(fp32), Wt[:, DS(t0, HALF_T)]))
                                        need(a)
                                        e.sem_inc(q_i, 1)
                                assert n == NV, n
                            if beside:
                                layernorm_relu(e, acc64)

                        @block.tensor
                        @guarded
                        def _(e):
                            e.sem_inc(q_r, 1)
                            with e.Fori(0, S_TURNS) as i:
                                for g in range(SB_GROUPS):
                                    b = g % 2
                                    e.wait_ge(q_oh, i * SB_GROUPS + g + 1)
                                    flat = oh[b][:, :, :].rearrange("p g d -> p (g d)")
                                    e.matmul(R[b][:, :], lhsT=U[:, :], rhs=flat, start=True, stop=True)
                                    for k in range(GRP - 1):
                                        m = GRP - 1 - k
                                        e.matmul(R[b][:, (k + 1) * P:], lhsT=ones[:, :],
                                                 rhs=oh[b][:, k:k + 1, :].to_broadcast([P, m, P]), start=False, stop=True,
                                                 skip_group_check=True)
                                    for k in range(GRP):
                                        last = e.matmul(T[b][:, 0:P], lhsT=ones[:, :], rhs=oh[b][:, k, :], start=k == 0, stop=k == GRP - 1)
                                    last.then_inc(q_r, 1)

                        @block.gpsimd
                        @guarded
                        def _(e):
                            for h in range(2):
                                e.dma_start(scr[h][:, :], src[0:16].rearrange("(a n) -> a n", a=1)).then_inc(q_s[h], 16)
                            with e.Fori(0, S_TURNS) as i:
                                for h in range(2):
                                    wait_here(e, q_i, i * 2 + h + 1)
                                    for t in range(HALF_T):
                                        e.indirect_dma_start(recs[key], bass.IndirectOffsetOnAxis(ap=idx[h][:, t:t + 1], axis=0),
                                                             rec[h][:, t, :], None).then_inc(q_s[h], 16)
                            for h in range(2):
                                e.wait_ge(q_s[h], S_TURNS * HALF_T * 16 + 16)

                        if beside:
                            beside(block)

            z1 = [sem(f"z1{h}") for h in range(2)]

            def runs(block):
                def half(e, h):
                    regs = [e.alloc_register(f"rr{h}_{n}") for n in range(HT)]
                    with e.Fori(0, TURNS) as i:
                        e.load(regs, e0s[h][0:1, DS(i * BODY + h * HT, HT)])
                        for t in range(HT):
                            o = e.snap(regs[t], min_val=0, max_val=EP)
                            e.dma_start(recT[DS(i * BODY + (h * HT + t), 1), :], SD[0:1, DS(o * 2, 2 * P)]).then_inc(z1[h], 16)
                    e.wait_ge(z1[h], NT // 2 * 16)

                @block.sync
                def _(e):
                    half(e, 0)
                    e.wait_ge(s_n, 8)
                    e.dma_start(tab_h.rearrange("(b p) f -> p b f", p=P), Hn).then_inc(s_h0, 16)
                    e.wait_ge(s_h0, 16)

                @block.scalar
                def _(e):
                    half(e, 1)
                    ln_act(e, 5)

            na[0] += 1
            sort("s", "d", None, runs)

            tx = ExitStack()
            with tx:
                TR = [sbt(tx, f"TR{n}", [P, P, 2], i32) for n in range(2)]
                TF = [sbt(tx, f"TF{n}", [P, 2, P], fp32) for n in range(2)]
                RD = [sbt(tx, f"RD{n}", [P, P, 4], i32) for n in range(2)]
                b128 = sbt(tx, "b128", [P, NC], fp32)
                pq = [pst(tx, f"pq{n}") for n in range(2)]
                t_l, t_f, t_p, t_r, t_s = sem("t_l0"), sem("t_f"), sem("t_p"), sem("t_r"), [sem("t_s0"), sem("t_s1")]
                t_l = [t_l, sem("t_l1")]
                rv = recs["d"].rearrange("(s t) c -> s t c", s=P)
                with nc.Block() as block:
                    @block.sync
                    def _(e):
                        for c in range(NC + 1):
                            if c < NC:
                                if c >= 2:
                                    e.wait_ge(t_f, c)
                                e.dma_start(TR[c % 2][:, :, :], recT[c * P:(c + 1) * P, :].rearrange("t (s c) -> t s c", c=2)).then_inc(t_l[c % 2], 16)
                            if c >= 1:
                                q = c - 1
                                e.wait_ge(t_r, 2 * q + 4)
                                e.dma_start(rv[:, q * P:(q + 1) * P, :], RD[q % 2][:, :, :]).then_inc(t_s[q % 2], 16)
                        for h in range(2):
                            e.wait_ge(t_s[h], NC // 2 * 16)

                    @block.vector
                    def _(e):
                        e.memset(RD[0][:, :, :], 0).then_inc(t_r, 1)
                        e.memset(RD[1][:, :, :], 0).then_inc(t_r, 1)
                        e.wait_ge(t_r, 2)
                        e.tensor_scalar(b128[:, :], bT["d"][:, :], 128.0, None, ALU.mult).then_inc(t_f, 1)
                        e.wait_ge(t_f, 1)
                        for c in range(NC + 1):
                            if c < NC:
                                e.wait_ge(t_l[c % 2], (c // 2 + 1) * 16)
                                if c >= 2:
                                    e.wait_ge(t_p, c - 1)
                                e.tensor_copy(TF[c % 2][:, 0, :], TR[c % 2][:, :, 0])
                                e.tensor_scalar(TF[c % 2][:, 1, :], TR[c % 2][:, :, 1], b128[:, c:c + 1], None, ALU.subtract).then_inc(t_f, 1)
                            if c >= 1:
                                q = c - 1
                                e.wait_ge(t_p, q + 1)
                                if q >= 2:
                                    e.wait_ge(t_s[q % 2], (q // 2) * 16)
                                e.tensor_copy(RD[q % 2][:, :, 0], pq[q % 2][:, 0:P]).then_inc(t_r, 1)
                                e.tensor_copy(RD[q % 2][:, :, 1].bitcast(fp32), pq[q % 2][:, P:2 * P]).then_inc(t_r, 1)

                    @block.tensor
                    def _(e):
                        for c in range(NC):
                            e.wait_ge(t_f, c + 2)
                            if c >= 2:
                                e.wait_ge(t_r, 2 * (c - 2) + 4)
                            e.transpose(pq[c % 2][:, 0:P], TF[c % 2][:, 0, :], idn[:, :])
                            e.transpose(pq[c % 2][:, P:2 * P], TF[c % 2][:, 1, :], idn[:, :]).then_inc(t_p, 1)

            z2 = sem("z2")

            def general(e):
                return e.value_load(badi[0:1, 0:1], min_val=0, max_val=1)

            with nc.Block() as block:
                @block.sync
                def _(e):
                    with e.If(general(e)):
                        v = recs["d"].rearrange("(p t) c -> p t c", p=P)
                        for j in range(8):
                            e.dma_start(v[:, j * 416:(j + 1) * 416, :], fill[:, :, :]).then_inc(z2, 16)
                        e.wait_ge(z2, 128)
            sort("d", "s", general)

        def load_rows(name, a, n):
            t = sbt(root, name, [P, n], fp32)
            return t, a.rearrange("(a n) -> a n", a=1).to_broadcast([P, n])

        nW = {}
        loads = []
        for name, a, k, n in (("W1s", W1, F, F), ("W2s", W2, F, F), ("eW1a", eW1[0:F, :], F, HID), ("eW1b", eW1[F:2 * F, :], F, HID),
                              ("eW2s", eW2, HID, HID), ("nW1a", nW1[0:F, :], F, HID), ("nW1b", nW1[F:F + HID, :], HID, HID),
                              ("nW2s", nW2, HID, F)):
            nW[name] = sbt(root, name, [k, n], fp32)
            loads.append((nW[name][:, :], a))
        for name, a, n in (("b1s", b1, F), ("b2s", b2, F), ("nb2s", nb2, F), ("eb2s", eb2, HID),
                           ("w1b", eW1[2 * F:2 * F + 1, :].rearrange("a n -> (a n)"), HID)):
            nW[name], v = load_rows(name, a, n)
            loads.append((nW[name][:, :], v))
        for name, a in (("eb1s", eb1), ("nb1s", nb1)):
            nW[name] = sbt(root, name, [HID, 1], fp32)
            loads.append((nW[name][:, :], a.rearrange("(n a) -> n a", a=1)))

        with nc.Block() as block:
            @block.scalar
            def _(e):
                for o, a in loads:
                    e.dma_start(o, a).then_inc(s_w, 16)
                e.wait_ge(s_w, 16 * len(loads))

        s_rec = [sem(f"s_rec{h}") for h in range(2)]
        s_g = [sem(f"s_g{k}") for k in range(BODY)]
        s_oh, s_pe, s_add, s_pre = sem("s_oh"), sem("s_pe"), sem("s_add"), sem("s_pre")
        nhop = [0]

        def hop(table, k, count=False):
            W = F + 1 if count else F
            r = nhop[0]
            nhop[0] += 1
            rv = recs[k].rearrange("(s t) c -> s t c", s=P)
            b_rec, b_g, b_oh, b_pe, b_add = r * TURNS * 32, r * TURNS * 16, r * TURNS * 2, r * TURNS * 8, r * (TURNS * BODY + 17)
            cx = ExitStack()
            with cx:
                G = sbt(cx, f"G{r}", [P, BODY, W], fp32)
                rb = [sbt(cx, f"rb{r}{h}", [P, HT, 4], i32) for h in range(2)]
                tb = [sbt(cx, f"tb{r}{h}", [1, HT], i32) for h in range(2)]
                O = [sbt(cx, f"O{r}{h}", [P, HT, P], fp32) for h in range(2)]
                ps = [pst(cx, f"ps{r}{b}") for b in range(8)]
                with nc.Block() as block:
                    @block.sync
                    def _(e):
                        with e.Fori(0, TURNS) as i:
                            for h in range(2):
                                e.wait_ge(s_add, i * BODY + (b_add + 1 + h * HT))
                                e.dma_start(rb[h][:, :, :], rv[:, DS(i * BODY + h * HT, HT), :]).then_inc(s_rec[h], 16)
                                e.dma_start(tb[h][:, :], tofs[k][DS(i * 2 + h, 1), :]).then_inc(s_rec[h], 16)

                    @block.gpsimd
                    def _(e):
                        with e.Fori(0, TURNS) as i:
                            for h in range(2):
                                wait_here(e, s_rec[h], i * 32 + (b_rec + 32))
                                for t in range(HT):
                                    s = h * HT + t
                                    e.indirect_dma_start(G[:, s, 0:F], None, table,
                                                         bass.IndirectOffsetOnAxis(ap=rb[h][:, t, 0:1], axis=0)).then_inc(s_g[s], 16)

                    @block.tensor
                    def _(e):
                        with e.Fori(0, TURNS) as i:
                            for h in range(2):
                                e.wait_ge(s_oh, i * 2 + (b_oh + h + 1))
                                for t in range(HT):
                                    s = h * HT + t
                                    e.wait_ge(s_g[s], i * 16 + (b_g + 16))
                                    ins = e.matmul(ps[s // 4][:, (s % 4) * W:(s % 4 + 1) * W], lhsT=O[h][:, t, :], rhs=G[:, s, :],
                                                   start=True, stop=True)
                                    if s % 4 == 3:
                                        ins.then_inc(s_pe, 1)

                    @block.vector
                    def _(e):
                        e.memset(ACC[:, 0:NB * W], 0.0).then_inc(s_add, 17)
                        if count:
                            e.memset(G[:, :, F:W], 1.0)
                        regs = [e.alloc_register(f"hr{r}_{n}") for n in range(HT)]
                        with e.Fori(0, TURNS) as i:
                            def onehot(h):
                                e.wait_ge(s_rec[h], i * 32 + (b_rec + 32))
                                e.tensor_tensor(O[h][:, :, :], rb[h][:, :, 1:2].bitcast(fp32).to_broadcast([P, HT, P]),
                                                iota[:, :].unsqueeze(1).to_broadcast([P, HT, P]), ALU.is_equal).then_inc(s_oh, 1)

                            onehot(0)
                            for h in range(2):
                                if h == 0:
                                    onehot(1)
                                e.load(regs, tb[h][0:1, :])
                                for t in range(HT):
                                    s = h * HT + t
                                    if s % 4 == 0:
                                        e.wait_ge(s_pe, i * 8 + (b_pe + s // 4 + 1))
                                    o = e.snap(regs[t], min_val=0, max_val=NB - 1)
                                    e.wait_ge(s_add, i * BODY + (b_add + 17 + s))
                                    e.tensor_tensor(ACC[:, DS(o * W, W)], ACC[:, DS(o * W, W)], ps[s // 4][:, (s % 4) * W:(s % 4 + 1) * W],
                                                    ALU.add).then_inc(s_add, 1)

        def scale(e, k, count):
            acc = acc65 if count else acc64
            if count:
                for step in (lambda: e.tensor_scalar(cinv[k][:, :], acc65[:, :, F], 1.0, None, ALU.max),
                             lambda: e.reciprocal(cinv[k][:, :], cinv[k][:, :])):
                    nn[0] += 1
                    step().then_inc(s_n, 1)
                    e.wait_ge(s_n, nn[0])
            nn[0] += 1
            e.tensor_tensor(Hn, acc[:, :, 0:F], cinv[k][:, :].unsqueeze(2).to_broadcast([P, NB, F]), ALU.mult).then_inc(s_n, 1)

        def scale_store(k, table, count=False):
            w = nst[0]
            nst[0] += 16
            with nc.Block() as block:
                @block.vector
                def _(e):
                    scale(e, k, count)

                @block.sync
                def _(e):
                    e.wait_ge(s_n, nn[0])
                    e.dma_start(table.rearrange("(b p) f -> p b f", p=P), Hn).then_inc(s_w2, 16)
                    e.wait_ge(s_w2, w + 16)

        s_w2 = sem("s_w2")
        nst = [0]
        s_t, s_tc, s_m, s_o = sem("s_t"), sem("s_tc"), sem("s_m"), sem("s_o")
        GB = 4
        NG = NB // GB
        nlin = [0]

        def linear(name, w, finish):
            r = nlin[0]
            nlin[0] += 1
            b = r * NG
            cx = ExitStack()
            with cx:
                pt = [pst(cx, f"pt{name}{n}") for n in range(2)]
                po = [pst(cx, f"po{name}{n}") for n in range(2)]
                hT = [sbt(cx, f"hT{name}{n}", [F, GB, P], fp32) for n in range(2)]
                n = w.shape[1]
                with nc.Block() as block:
                    @block.tensor
                    def _(e):
                        for g in range(NG + 1):
                            if g < NG:
                                if g >= 2:
                                    e.wait_ge(s_tc, b + g - 1)
                                for j in range(GB):
                                    ins = e.transpose(pt[g % 2][0:F, j * P:(j + 1) * P], Hn[:, g * GB + j, :], idn[:, :])
                                ins.then_inc(s_t, 1)
                            if g >= 1:
                                q = g - 1
                                e.wait_ge(s_tc, b + q + 1)
                                if q >= 2:
                                    e.wait_ge(s_o, b + q - 1)
                                for j in range(GB):
                                    ins = e.matmul(po[q % 2][:, j * n:(j + 1) * n], lhsT=hT[q % 2][:, j, :], rhs=w[:, :], start=True, stop=True)
                                ins.then_inc(s_m, 1)

                    @block.scalar
                    def _(e):
                        for g in range(NG):
                            e.wait_ge(s_t, b + g + 1)
                            if g >= 2:
                                e.wait_ge(s_m, b + g - 1)
                            e.activation(hT[g % 2][:, :, :].rearrange("p j n -> p (j n)"), pt[g % 2][0:F, :], ACT.Copy).then_inc(s_tc, 1)

                    @block.vector
                    def _(e):
                        for g in range(NG):
                            e.wait_ge(s_m, b + g + 1)
                            finish(e, g, po[g % 2][:, 0:GB * n].rearrange("p (j n) -> p j n", n=n)).then_inc(s_o, 1)

        def bc(t, n):
            return t[:, :].unsqueeze(1).to_broadcast([P, GB, n])

        def store_block(table, v):
            w = nst[0]
            nst[0] += 16
            with nc.Block() as block:
                @block.sync
                def _(e):
                    e.dma_start(table.rearrange("(b p) f -> p b f", p=P), v).then_inc(s_w2, 16)
                    e.wait_ge(s_w2, w + 16)

        hop(tab_h, "d", True)
        scale_store("d", tab_e, True)
        hop(tab_e, "s", True)
        with nc.Block() as block:
            @block.vector
            def _(e):
                scale(e, "s", True)

        linear("a", nW["W1s"], lambda e, g, p: e.tensor_tensor(acc64[:, g * GB:(g + 1) * GB, :], p, bc(nW["b1s"], F), ALU.add))
        nn[0] += 1
        with nc.Block() as block:
            @block.vector
            def _(e):
                e.tensor_scalar(Hn, acc64, 0.0, None, ALU.max).then_inc(s_n, 1)
        store_block(tab_h, Hn)
        hop(tab_h, "d")
        scale_store("d", tab_e)
        hop(tab_e, "s")
        with nc.Block() as block:
            @block.vector
            def _(e):
                scale(e, "s", False)

        linear("b", nW["W2s"], lambda e, g, p: e.tensor_tensor(acc64[:, g * GB:(g + 1) * GB, :], p, bc(nW["b2s"], F), ALU.add))
        n0 = nn[0]
        nn[0] += 1
        with nc.Block() as block:
            na[0] += 1

            @block.scalar
            def _(e):
                ln_act(e, n0 + 6)

            @block.vector
            def _(e):
                e.tensor_tensor(X[:, :, :], X[:, :, :], acc64, ALU.add).then_inc(s_n, 1)
                e.wait_ge(s_n, n0 + 1)
                layernorm_relu(e, acc64)

        tab_n = dram("tab_n", (ROWS, F), fp32)
        tab_x = dram("tab_x", (ROWS, F), fp32)
        store_block(tab_n, Hn)
        store_block(tab_x, X[:, :, :])
        qx = ExitStack()
        with qx:
            Qt = sbt(qx, "Qt", [P, NB, HID], fp32)
            linear("q", nW["eW1b"], lambda e, g, p: e.tensor_copy(Qt[:, g * GB:(g + 1) * GB, :], p))
            store_block(tab_q, Qt[:, :, :])
        big = ExitStack()
        with big:
            P3 = sbt(big, "P3", [P, NB, 3, HID], bf16)
            px = ExitStack()
            with px:
                rem = [sbt(px, f"rem{n}", [P, GB, HID], fp32) for n in range(2)]
                s_sp = sem("s_sp")
                nsp = [0]

                def split(e, g, p):
                    def link(ins):
                        nsp[0] += 1
                        ins.then_inc(s_sp, 1)
                        e.wait_ge(s_sp, nsp[0])

                    bs = slice(g * GB, (g + 1) * GB)
                    link(e.tensor_copy(P3[:, bs, 0, :], p))
                    link(e.tensor_tensor(rem[0][:, :, :], p, P3[:, bs, 0, :], ALU.subtract))
                    link(e.tensor_copy(P3[:, bs, 1, :], rem[0][:, :, :]))
                    link(e.tensor_tensor(rem[1][:, :, :], rem[0][:, :, :], P3[:, bs, 1, :], ALU.subtract))
                    return e.tensor_copy(P3[:, bs, 2, :], rem[1][:, :, :])

                linear("p", nW["eW1a"], split)

            LQ, LT = 4, BODY // 4
            l_rec = [sem(f"l_rec{h}") for h in range(LQ)]
            l_oh, l_ob, l_w, l_t, l_tc, l_p, l_y, l_2, l_zb, l_z, l_a, l_add = (
                sem(f"l_{n}") for n in ("oh", "ob", "w", "t", "tc", "p", "y", "2", "zb", "z", "a", "add"))
            b_g = nhop[0] * TURNS * 16
            CR = BODY - LT + 1
            tofl = tofs["s"].rearrange("a (h t) -> (a h) t", t=LT)
            rv = recs["s"].rearrange("(s t) c -> s t c", s=P)
            cx = ExitStack()
            with cx:
                G = sbt(cx, "GL", [P, BODY, HID], fp32)
                rb = [sbt(cx, f"rbL{h}", [P, LT, 4], i32) for h in range(LQ)]
                tb = [sbt(cx, f"tbL{h}", [1, LT], i32) for h in range(LQ)]
                O = [sbt(cx, f"OL{h}", [P, LT, P], fp32) for h in range(LQ)]
                ST = [sbt(cx, f"ST{n}", [P, 512], bf16) for n in range(2)]
                Ob = [X[:, LT * h:LT * h + LT, :].bitcast(bf16) for h in range(LQ)]
                Y = sbt(cx, "Y", [P, 512], fp32)
                Zb = sbt(cx, "Zb", [P, 512], fp32)
                Z = sbt(cx, "Z", [P, 512], fp32)
                pT = [pst(cx, f"pT{n}", bf16) for n in range(2)]
                pP = [pst(cx, f"pP{n}") for n in range(2)]
                p2 = [pst(cx, f"p2{n}") for n in range(2)]
                pA = [pst(cx, f"pA{n}") for n in range(2)]
                Pf = P3[:, :, :, :].rearrange("p b c h -> p (b c h)")
                NGL = BODY // 4

                def done(e, s, i, g):
                    e.wait_ge(s, i * NGL + (g + 3))

                def skewed(e, slots):
                    depth = max(n for slot in slots for n, _ in slot)

                    def turn(i, first, last):
                        for g in range(depth if last else NGL):
                            for slot in slots:
                                steps = [f(i, g - n) for n, f in slot if (g >= n or not first) and (g < n or not last)]
                                while steps:
                                    steps = [x for x in steps if next(x, None)]

                    turn(0, True, False)
                    with e.Fori(1, TURNS) as i:
                        turn(i, False, False)
                    turn(TURNS, False, True)

                with nc.Block() as block:
                    @block.sync
                    def _(e):
                        with e.Fori(0, TURNS) as i:
                            for h in range(LQ):
                                e.wait_ge(l_add, i * BODY + (CR - BODY + (h + 1) * LT))
                                e.dma_start(rb[h][:, :, :], rv[:, DS(i * BODY + h * LT, LT), :]).then_inc(l_rec[h], 16)
                                e.dma_start(tb[h][:, :], tofl[DS(i * LQ + h, 1), :]).then_inc(l_rec[h], 16)

                    @block.gpsimd
                    def _(e):
                        with e.Fori(0, TURNS) as i:
                            for h in range(LQ):
                                wait_here(e, l_rec[h], i * 32 + 32)
                                for t in range(LT):
                                    s = h * LT + t
                                    e.indirect_dma_start(G[:, s, :], None, tab_q,
                                                         bass.IndirectOffsetOnAxis(ap=rb[h][:, t, 0:1], axis=0)).then_inc(s_g[s], 16)

                    @block.tensor
                    def _(e):
                        for s in (l_t, l_p, l_2, l_a):
                            e.sem_inc(s, 2)
                        regs = [e.alloc_register(f"lp_{n}") for n in range(LT)]

                        def stage_t(i, g):
                            if g % 2 == 0:
                                e.wait_ge(l_ob, i * LQ + (g // 2 + 1))
                            done(e, l_tc, i, g - 2)
                            for j in range(4):
                                ins = e.transpose(pT[g % 2][:, j * P:(j + 1) * P], Ob[g % NGL // 2][:, (g % 2) * 4 + j, :], idb[:, :])
                            ins.then_inc(l_t, 1)
                            yield True

                        def stage_p(i, g):
                            if g % 2 == 0:
                                e.load(regs, tb[g % NGL // 2][0:1, :])
                            done(e, l_tc, i, g)
                            done(e, l_w, i, g)
                            done(e, l_y, i, g - 2)
                            for j in range(4):
                                s = g % NGL * 4 + j
                                o = e.snap(regs[s % LT], min_val=0, max_val=NB - 1)
                                for c in range(3):
                                    e.matmul(pP[g % 2][:, j * P:(j + 1) * P], lhsT=Pf[:, DS(o * (3 * HID) + c * HID, HID)],
                                             rhs=ST[g % 2][:, j * P:(j + 1) * P], start=c == 0, stop=False)
                                ins = e.matmul(pP[g % 2][:, j * P:(j + 1) * P], lhsT=G[:, s, :], rhs=idn[:, :], start=False, stop=True)
                            ins.then_inc(l_p, 1)
                            yield True

                        def stage_2(i, g):
                            done(e, l_y, i, g)
                            done(e, l_zb, i, g - 2)
                            for j in range(4):
                                ins = e.matmul(p2[g % 2][:, j * P:(j + 1) * P], lhsT=Y[:, j * P:(j + 1) * P], rhs=nW["eW2s"][:, :],
                                               start=True, stop=True)
                            ins.then_inc(l_2, 1)
                            yield True

                        def stage_a(i, g):
                            done(e, l_z, i, g)
                            e.wait_ge(l_add, i * BODY + (CR + g * 4 - 4))
                            for j in range(4):
                                s = g % NGL * 4 + j
                                ins = e.matmul(pA[g % 2][:, j * P:(j + 1) * P], lhsT=O[s // LT][:, s % LT, :],
                                               rhs=Z[:, j * P:(j + 1) * P], start=True, stop=True)
                            ins.then_inc(l_a, 1)
                            yield True

                        skewed(e, [[(2, stage_t)], [(3, stage_p)], [(4, stage_2)], [(5, stage_a)]])

                    @block.scalar
                    def _(e):
                        for s in (l_tc, l_y, l_z):
                            e.sem_inc(s, 2)

                        def cast(i, g):
                            if g % 2 == 0:
                                e.wait_ge(l_oh, i * LQ + (g // 2 + 1))
                                e.activation(Ob[g // 2], O[g // 2][:, :, :], ACT.Copy).then_inc(l_ob, 1)
                            yield True

                        def copy_t(i, g):
                            done(e, l_t, i, g)
                            done(e, l_p, i, g - 2)
                            e.activation(ST[g % 2][:, :], pT[g % 2][:, 0:512], ACT.Copy).then_inc(l_tc, 1)
                            yield True

                        def silu_1(i, g):
                            done(e, l_p, i, g)
                            done(e, l_2, i, g - 1)
                            e.activation(Y[:, :], pP[g % 2][:, :], ACT.Silu, bias=nW["eb1s"][:, 0:1]).then_inc(l_y, 1)
                            yield True

                        def silu_2(i, g):
                            done(e, l_zb, i, g)
                            done(e, l_a, i, g - 1)
                            e.activation(Z[:, :], Zb[:, :], ACT.Silu).then_inc(l_z, 1)
                            yield True

                        skewed(e, [[(2, copy_t)], [(3, silu_1)], [(4, silu_2)], [(0, cast)]])

                    @block.vector
                    def _(e):
                        e.memset(ACC[:, 0:NB * HID], 0.0).then_inc(l_add, CR)
                        e.sem_inc(l_zb, 2)
                        e.sem_inc(l_w, 2)
                        regs = [e.alloc_register(f"la_{n}") for n in range(LT)]

                        def onehot(i, g):
                            h = g // 2
                            if g % 2 == 0:
                                e.wait_ge(l_rec[h], i * 32 + 32)
                                e.tensor_tensor(O[h][:, :, :], rb[h][:, :, 1:2].bitcast(fp32).to_broadcast([P, LT, P]),
                                                iota[:, :].unsqueeze(1).to_broadcast([P, LT, P]), ALU.is_equal).then_inc(l_oh, 1)
                            yield True

                        def weight(i, g):
                            for j in range(4):
                                s = g % NGL * 4 + j
                                e.wait_ge(s_g[s], i * 16 + (b_g + (16 if g >= 0 else 0)))
                                ins = e.scalar_tensor_tensor(G[:, s, :], nW["w1b"][:, :], rb[s // LT][:, s % LT, 2:3].bitcast(fp32),
                                                             G[:, s, :], ALU.mult, ALU.add)
                                if j == 3:
                                    ins.then_inc(l_w, 1)
                                yield True

                        def bias2(i, g):
                            done(e, l_2, i, g)
                            done(e, l_z, i, g - 1)
                            e.tensor_tensor(Zb[:, :].rearrange("p (j n) -> p j n", n=HID), p2[g % 2][:, :].rearrange("p (j n) -> p j n", n=HID),
                                            nW["eb2s"][:, :].unsqueeze(1).to_broadcast([P, 4, HID]), ALU.add).then_inc(l_zb, 1)
                            yield True

                        def add(i, g):
                            if g % 2 == 0:
                                e.load(regs, tb[g % NGL // 2][0:1, :])
                            done(e, l_a, i, g)
                            for j in range(4):
                                s = g % NGL * 4 + j
                                o = e.snap(regs[s % LT], min_val=0, max_val=NB - 1)
                                e.wait_ge(l_add, i * BODY + (CR + g * 4 + j))
                                e.tensor_tensor(ACC[:, DS(o * HID, HID)], ACC[:, DS(o * HID, HID)], pA[g % 2][:, j * P:(j + 1) * P],
                                                ALU.add).then_inc(l_add, 1)
                                yield True

                        skewed(e, [[(4, bias2)], [(5, add), (1, weight)], [(0, onehot)]])

        fx = ExitStack()
        with fx:
            H1 = sbt(fx, "H1", [P, NB, F], fp32)
            OUT = sbt(fx, "OUT", [P, NB, F], fp32)
            hT = [sbt(fx, f"fhT{n}", [F, 512], fp32) for n in range(2)]
            aT = [sbt(fx, f"faT{n}", [P, 512], fp32) for n in range(2)]
            u = [sbt(fx, f"fu{n}", [P, 512], fp32) for n in range(2)]
            ph = pst(fx, "ph")
            pa = pst(fx, "pa")
            pu = [pst(fx, f"pu{n}") for n in range(2)]
            po = [pst(fx, f"pof{n}") for n in range(2)]
            f_x, f_l, f_t, f_hc, f_ac, f_u, f_s, f_o, f_v, f_b = (sem(f"f_{n}") for n in ("x", "l", "t", "hc", "ac", "u", "s", "o", "v", "b"))
            with nc.Block() as block:
                @block.sync
                def _(e):
                    e.dma_start(H1[:, :, :], tab_n.rearrange("(b p) f -> p b f", p=P)).then_inc(f_l, 16)
                    e.dma_start(X[:, :, :], tab_x.rearrange("(b p) f -> p b f", p=P)).then_inc(f_x, 16)
                    e.wait_ge(f_v, NG)
                    e.dma_start(out[0:97 * P, :].rearrange("(b p) f -> p b f", p=P), OUT[:, 0:97, :]).then_inc(f_l, 16)
                    e.dma_start(out[97 * P:N_NODES, :], OUT[0:N_NODES - 97 * P, 97, :]).then_inc(f_l, 16)
                    e.wait_ge(f_l, 48)

                @block.tensor
                def _(e):
                    e.wait_ge(f_l, 16)
                    for g in range(NG + 2):
                        if g < NG:
                            e.wait_ge(f_hc, g)
                            e.wait_ge(f_ac, g)
                            for j in range(GB):
                                e.transpose(ph[0:F, j * P:(j + 1) * P], H1[:, g * GB + j, :], idn[:, :])
                                ins = e.transpose(pa[:, j * P:(j + 1) * P], ACC[:, (g * GB + j) * HID:(g * GB + j + 1) * HID], idn[:, :])
                            ins.then_inc(f_t, 1)
                        if 1 <= g <= NG:
                            q = g - 1
                            e.wait_ge(f_hc, q + 1)
                            e.wait_ge(f_ac, q + 1)
                            if q >= 2:
                                e.wait_ge(f_s, q - 1)
                            e.matmul(pu[q % 2][:, :], lhsT=nW["nW1a"][:, :], rhs=hT[q % 2][:, :], start=True, stop=False)
                            e.matmul(pu[q % 2][:, :], lhsT=nW["nW1b"][:, :], rhs=aT[q % 2][:, :], start=False, stop=True).then_inc(f_u, 1)
                        if 2 <= g:
                            q = g - 2
                            e.wait_ge(f_s, q + 1)
                            if q >= 2:
                                e.wait_ge(f_v, q - 1)
                            for j in range(GB):
                                ins = e.matmul(po[q % 2][:, j * F:(j + 1) * F], lhsT=u[q % 2][:, j * P:(j + 1) * P], rhs=nW["nW2s"][:, :],
                                               start=True, stop=True)
                            ins.then_inc(f_o, 1)

                @block.scalar
                def _(e):
                    for g in range(NG + 1):
                        if g < NG:
                            e.wait_ge(f_t, g + 1)
                            if g >= 2:
                                e.wait_ge(f_u, g - 1)
                            e.activation(hT[g % 2][:, :], ph[0:F, :], ACT.Copy).then_inc(f_hc, 1)
                        if g >= 1:
                            q = g - 1
                            e.wait_ge(f_u, q + 1)
                            if q >= 2:
                                e.wait_ge(f_o, q - 1)
                            e.activation(u[q % 2][:, :], pu[q % 2][:, :], ACT.Silu, bias=nW["nb1s"][:, 0:1]).then_inc(f_s, 1)

                @block.vector
                def _(e):
                    e.wait_ge(f_x, 16)
                    for g in range(NG + 2):
                        if g < NG:
                            e.wait_ge(f_t, g + 1)
                            if g >= 2:
                                e.wait_ge(f_u, g - 1)
                            e.tensor_copy(aT[g % 2][:, :], pa[:, :]).then_inc(f_ac, 1)
                        if g >= 2:
                            q = g - 2
                            v = OUT[:, q * GB:(q + 1) * GB, :]
                            e.wait_ge(f_o, q + 1)
                            e.tensor_tensor(v, po[q % 2][:, 0:GB * F].rearrange("p (j n) -> p j n", n=F), bc(nW["nb2s"], F),
                                            ALU.add).then_inc(f_b, 1)
                            e.wait_ge(f_b, q + 1)
                            e.tensor_tensor(v, v, X[:, q * GB:(q + 1) * GB, :], ALU.add).then_inc(f_v, 1)


_INS = ['x', 'src', 'dst', 'edge_weight1', 'L0_gnn_W1', 'L0_gnn_b1', 'L0_gnn_W2', 'L0_gnn_b2', 'L1_gnn_eW1', 'L1_gnn_eb1',
        'L1_gnn_eW2', 'L1_gnn_eb2', 'L1_gnn_nW1', 'L1_gnn_nb1', 'L1_gnn_nW2', 'L1_gnn_nb2']


def kernel(**inputs):
    import numpy as np
    import concourse.bacc as bacc
    from concourse import mybir as mb
    from concourse.bass_utils import run_bass_kernel_spmd

    nc = bacc.Bacc("TRN2", target_bir_lowering=False, num_devices=1)
    arrays, args = {}, []
    for name in _INS:
        a = np.ascontiguousarray(inputs[name])
        if name == "edge_weight1":
            a = a.reshape(N_EDGES)
        arrays[f"in_{name}"] = a
        args.append(nc.dram_tensor(f"in_{name}", a.shape, mb.dt.from_np(a.dtype), kind="ExternalInput").ap())
    args.append(nc.dram_tensor("out_0", (N_NODES, F), mb.dt.float32, kind="ExternalOutput").ap())
    gnn_kernel(nc, *args)
    r = run_bass_kernel_spmd(nc, [arrays], core_ids=[0])
    return r.results[0]["out_0"]
```
